# Optimizing a Trainium2 kernel written in Bass

```python
import numpy as np
import jax
import jax.numpy as jnp

def _softmax(x, axis=-1):
    return jax.nn.softmax(x, axis=axis)

def _gelu(x):
    return jax.nn.gelu(x, approximate=True)

def _silu(x):
    return jax.nn.silu(x)

def _sigmoid(x):
    return jax.nn.sigmoid(x)

def _layernorm(x, axis=-1, eps=1e-05):
    m = jnp.mean(x, axis=axis, keepdims=True)
    v = jnp.var(x, axis=axis, keepdims=True)
    return (x - m) / jnp.sqrt(v + eps)

def _scatter_add(tgt, idx, src, axis=0):
    return tgt.at[idx].add(src)

def _segment_sum(src, seg, n):
    return jax.ops.segment_sum(src, seg, n)
kernel_name = 'mk_prb_d1_jaxref_r4_5bc7a8'

def setup_inputs(seed: int=0):
    np.random.seed(seed)
    _w = jnp.asarray

    def _L0_attn_setup():
        import jax, jax.numpy as jnp
        import numpy as np
        D_MODEL = 256
        N_HEADS = 16
        D_HEAD = D_MODEL // N_HEADS
        WIN = 64
        NEG_INF = -1e+30

        def _band_mask(nb: int):
            ti = jnp.arange(WIN)[:, None]
            tj = jnp.arange(2 * WIN)[None, :]
            base = (tj >= ti + 1) & (tj <= ti + WIN)
            first = base & (tj >= WIN)
            rest = jnp.broadcast_to(base, (nb - 1, WIN, 2 * WIN))
            return jnp.concatenate([first[None], rest], axis=0)
        key = jax.random.key(seed)
        k1, k2, k3 = jax.random.split(key, 3)
        B, L = (4, 1024)
        x = jax.random.normal(k1, (B, L, D_MODEL), dtype=jnp.float32)
        w_qkv = jax.random.normal(k2, (D_MODEL, 3 * D_MODEL), dtype=jnp.float32) * (1.0 / np.sqrt(D_MODEL))
        w_out = jax.random.normal(k3, (D_MODEL, D_MODEL), dtype=jnp.float32) * (1.0 / np.sqrt(D_MODEL))
        return {'x': x, 'w_qkv': w_qkv, 'w_out': w_out}
    _L0_attn_in = _L0_attn_setup()

    def _L0_ffn_setup():
        import jax, jax.numpy as jnp
        import numpy as np
        E = 8
        K = 2
        CAP_FACTOR = 1.0
        key = jax.random.key(seed)
        k0, k1, k2, k3 = jax.random.split(key, 4)
        B, S, M, H = (4, 512, 256, 1024)
        x = jax.random.normal(k0, (B, S, M), jnp.float32)
        wg = jax.random.normal(k1, (M, E), jnp.float32) * 0.02
        w1 = jax.random.normal(k2, (E, M, H), jnp.float32) * 0.02
        b1 = jnp.zeros((E, H), jnp.float32)
        w2 = jax.random.normal(k3, (E, H, M), jnp.float32) * 0.02
        b2 = jnp.zeros((E, M), jnp.float32)
        return {'x': x, 'wg': wg, 'w1': w1, 'b1': b1, 'w2': w2, 'b2': b2}
    _L0_ffn_in = _L0_ffn_setup()
    _d = {'L0_attn_x': _L0_attn_in['x'], 'L0_attn_w_qkv': _L0_attn_in['w_qkv'], 'L0_attn_w_out': _L0_attn_in['w_out'], 'L0_ffn_wg': _L0_ffn_in['wg'], 'L0_ffn_w1': _L0_ffn_in['w1'], 'L0_ffn_b1': _L0_ffn_in['b1'], 'L0_ffn_w2': _L0_ffn_in['w2'], 'L0_ffn_b2': _L0_ffn_in['b2']}
    _x0 = _d['L0_attn_x']
    _d['L0_attn_x'] = jax.random.normal(jax.random.fold_in(jax.random.key(seed), 1), (4, 1024, 256), dtype=_x0.dtype)
    del _x0
    return _d

def reference(L0_attn_x, L0_attn_w_qkv, L0_attn_w_out, L0_ffn_wg, L0_ffn_w1, L0_ffn_b1, L0_ffn_w2, L0_ffn_b2):

    def _L0_attn_ref(x, w_qkv, w_out):
        import jax, jax.numpy as jnp
        import numpy as np
        D_MODEL = 256
        N_HEADS = 16
        D_HEAD = D_MODEL // N_HEADS
        WIN = 64
        NEG_INF = -1e+30

        def _band_mask(nb: int):
            ti = jnp.arange(WIN)[:, None]
            tj = jnp.arange(2 * WIN)[None, :]
            base = (tj >= ti + 1) & (tj <= ti + WIN)
            first = base & (tj >= WIN)
            rest = jnp.broadcast_to(base, (nb - 1, WIN, 2 * WIN))
            return jnp.concatenate([first[None], rest], axis=0)
        B, L, D = x.shape
        nb = L // WIN
        qkv = (x @ w_qkv).reshape(B, L, 3, N_HEADS, D_HEAD)
        q, k, v = (qkv[:, :, 0], qkv[:, :, 1], qkv[:, :, 2])

        def to_blocks(t):
            return t.transpose(0, 2, 1, 3).reshape(B, N_HEADS, nb, WIN, D_HEAD)
        qb, kb, vb = (to_blocks(q), to_blocks(k), to_blocks(v))
        zero_blk = jnp.zeros_like(kb[:, :, :1])
        k_kv = jnp.concatenate([jnp.concatenate([zero_blk, kb[:, :, :-1]], axis=2), kb], axis=3)
        v_kv = jnp.concatenate([jnp.concatenate([zero_blk, vb[:, :, :-1]], axis=2), vb], axis=3)
        scale = 1.0 / np.sqrt(D_HEAD)
        scores = jnp.einsum('bhnqd,bhnkd->bhnqk', qb, k_kv) * scale
        scores = jnp.where(_band_mask(nb), scores, NEG_INF)
        attn = jax.nn.softmax(scores, axis=-1)
        ob = jnp.einsum('bhnqk,bhnkd->bhnqd', attn, v_kv)
        out = ob.reshape(B, N_HEADS, L, D_HEAD).transpose(0, 2, 1, 3).reshape(B, L, D)
        return out @ w_out

    def _L0_ffn_ref(x, wg, w1, b1, w2, b2):
        import jax, jax.numpy as jnp
        import numpy as np
        E = 8
        K = 2
        CAP_FACTOR = 1.0
        B, S, M = x.shape
        N = B * S
        capacity = int(CAP_FACTOR * K * N // E)
        xt = x.reshape(N, M)
        logits = xt @ wg
        scores = jax.nn.softmax(logits, axis=-1)
        topv, topi = jax.lax.top_k(scores, K)
        topv = topv / jnp.sum(topv, axis=-1, keepdims=True)
        masks = jax.nn.one_hot(topi.T, E, dtype=jnp.int32)
        flat = masks.reshape(K * N, E)
        locs = jnp.cumsum(flat, axis=0) - 1
        pos = jnp.sum(locs * flat, axis=-1).reshape(K, N).T
        valid = pos < capacity
        gate = topv * valid.astype(topv.dtype)
        pos_c = jnp.where(valid, pos, 0)
        xk = xt[:, None, :] * valid[..., None].astype(xt.dtype)
        disp = jnp.zeros((E, capacity, M), xt.dtype)
        disp = disp.at[topi, pos_c].add(xk)
        h = jax.nn.relu(jnp.einsum('ecm,emh->ech', disp, w1) + b1[:, None, :])
        y = jnp.einsum('ech,ehm->ecm', h, w2) + b2[:, None, :]
        out = jnp.sum(gate[..., None] * y[topi, pos_c], axis=1)
        return out.reshape(B, S, M)
    x = L0_attn_x
    xn = _layernorm(x, axis=-1)
    x = x + _L0_attn_ref(xn, L0_attn_w_qkv, L0_attn_w_out) + _L0_ffn_ref(xn, L0_ffn_wg, L0_ffn_w1, L0_ffn_b1, L0_ffn_w2, L0_ffn_b2)
    return x

_drawn_inputs = setup_inputs


def setup_inputs(seed=0):
    import zlib

    import numpy as np

    out = dict(_drawn_inputs(seed))
    spreads = {'L0_ffn_b1': (0.0, 0.1), 'L0_ffn_b2': (0.0, 0.1)}
    factors = {}
    for name, (base, spread) in spreads.items():
        noise = np.random.default_rng([zlib.crc32(name.encode()), seed]).standard_normal(out[name].shape)
        drawn = base * np.exp(spread * noise) if base else spread * noise
        out[name] = jnp.asarray(drawn.astype(out[name].dtype))
    for name, factor in factors.items():
        out[name] = (out[name] * factor).astype(out[name].dtype)
    return out
```

```python
import concourse.bass as bass
from concourse import mybir
from contextlib import ExitStack

fp32 = mybir.dt.float32
fp32r = mybir.dt.float32r
bf16 = mybir.dt.bfloat16
u32 = mybir.dt.uint32
i32 = mybir.dt.int32
ALU = mybir.AluOpType
ACT = mybir.ActivationFunctionType
AX = mybir.AxisListType

P = 128
B, L, D = 4, 1024, 256
N = B * L
KD = D // P
NT = N // P
E, K, H = 8, 2, 1024
CAP = K * N // E
HC = H // P
ST = CAP // P
HALF = CAP // 2
NH, DH, WIN = 16, 16, 64
NB = L // WIN
QUADS = NH // 4
NEG = -1e30
EPS = 1e-5
BIG = 3e38


class Mem:
    pass


def alone(eng, sem, value):
    eng.wait_ge(sem, value)
    eng.sem_inc(Mem.passed, 1)


def split_products(pe, out, pairs, n_start=True, n_stop=True):
    last, n = None, 3 * len(pairs)
    i = 0
    for lh, ll, rh, rl in pairs:
        for a, b in ((lh, rh), (lh, rl), (ll, rh)):
            last = pe.matmul(out, a, b, start=(n_start and i == 0), stop=(n_stop and i == n - 1))
            i += 1
    return last


def norm_phase(nc, m, x, xn_dram, wg, w_qkv, w_out, b1, b2):
    G = 4
    NG = NT // G
    ctx = ExitStack()
    with ctx:
        sb = lambda n, s, d: ctx.enter_context(nc.sbuf_tensor(n, s, d))
        sem = lambda n: ctx.enter_context(nc.semaphore(n))
        xin = sb("n_xin", [P, NT, D], fp32)
        xnb = sb("n_xn", [P, 2, G, D], fp32)
        stats = sb("n_stats", [P, NT, 6], fp32)
        mean, var, half_gap = (sb(f"n_{n}", [P, NT], fp32) for n in ("mean", "var", "gap"))
        std = sb("n_std", [P, NT], fp32)
        rstd = sb("n_rstd", [P, NT], fp32)
        eps = sb("n_eps", [P, 1], fp32)
        xT = sb("n_xT", [P, 2, KD, G * P], fp32)
        wgs = sb("n_wg", [P, KD, E], fp32)
        raw_qkv = sb("n_rawqkv", [P, KD, 3 * D], fp32)
        raw_out = sb("n_rawout", [P, QUADS, D], fp32)
        raw_b1 = sb("n_rawb1", [E * HC, P], fp32)
        psT = [ctx.enter_context(nc.psum_tensor(f"n_psT{i}", [P, G * P], fp32)) for i in range(4)]
        psL = ctx.enter_context(nc.psum_tensor("n_psL", [P, 512], fp32))
        psB = ctx.enter_context(nc.psum_tensor("n_psB", [P, 512], fp32))
        x_in = [sem(f"n_x_in{g}") for g in range(NG)]
        w_in = sem("n_w_in")
        wo_zero = sem("n_wo_zero")
        consts = sem("n_consts")
        made = sem("n_made")
        chain = sem("n_chain")
        var_done, std_done = sem("n_var_done"), sem("n_std_done")
        xn_done = [sem(f"n_xn_done{s}") for s in range(2)]
        xn_out = [sem(f"n_xn_out{s}") for s in range(2)]
        t_done = [sem(f"n_t_done{s}") for s in range(2)]
        xT_done = [sem(f"n_xT_done{s}") for s in range(2)]
        xT_used = [sem(f"n_xT_used{s}") for s in range(2)]
        hi_done = sem("n_hi_done")
        b1_t = sem("n_b1_t")
        xv = x.rearrange("b (t p) d -> p (b t) d", p=P)
        xnv = xn_dram.rearrange("(t p) d -> p t d", p=P)
        block = ctx.enter_context(nc.Block())

        @block.sync
        def _(sp):
            for g in range(NG):
                sp.dma_start(xin[:, g * G:(g + 1) * G], xv[:, g * G:(g + 1) * G, :]).then_inc(x_in[g], 16)
            with sp.Fori(0, NG // 2) as i:
                for s in range(2):
                    alone(sp, xn_done[s], G * (i + 1))
                    sp.dma_start(xnv[:, bass.ds((i * 2 + s) * G, G), :], xnb[:, s]).then_inc(xn_out[s], 16)
            for s in range(2):
                sp.wait_ge(xn_out[s], 16 * (NG // 2))

        @block.gpsimd
        def _(pool):
            pool.memset(m.eye[:, :], 0.0).then_inc(made, 1)
            pool.memset(raw_out[:, :, :], 0.0).then_inc(wo_zero, 1)
            pool.wait_ge(made, 1)
            pool.affine_select(out=m.eye[:, :], in_=m.eye[:, :], compare_op=ALU.not_equal, fill=1.0,
                               base=0, pattern=[[-1, P]], channel_multiplier=1).then_inc(consts, 1)
            pool.memset(m.mask[:, :, :], 0.0).then_inc(made, 1)
            n = 2
            for sign in (1, -1):
                pool.wait_ge(made, n)
                for first in range(2):
                    for s in range(2):
                        part = m.mask[s * WIN:(s + 1) * WIN, first, :]
                        pool.affine_select(out=part, in_=part, compare_op=ALU.is_ge, fill=NEG,
                                           base=-1 if sign == 1 else WIN, pattern=[[sign, 2 * WIN]],
                                           channel_multiplier=-sign).then_inc(made, 1)
                        n += 1
            pool.wait_ge(made, n)
            pool.memset(m.mask[:, 1, 0:WIN], NEG)

        @block.vector
        def _(dve):
            count = [0]

            def link(ins):
                count[0] += 1
                ins.then_inc(chain, 1)
                dve.wait_ge(chain, count[0])

            dve.memset(eps[:, :], EPS).then_inc(consts, 1)
            for g in range(NG):
                dve.wait_ge(x_in[g], 16)
                for j in range(g * G, (g + 1) * G):
                    ins = dve.bn_stats(stats[:, j, :], xin[:, j, :])
            link(ins)
            link(dve.tensor_tensor(mean[:, :], stats[:, :, 1], stats[:, :, 4], ALU.add))
            link(dve.tensor_tensor(half_gap[:, :], stats[:, :, 1], stats[:, :, 4], ALU.subtract))
            link(dve.tensor_tensor(half_gap[:, :], half_gap[:, :], half_gap[:, :], ALU.mult))
            link(dve.tensor_tensor(var[:, :], stats[:, :, 2], stats[:, :, 5], ALU.add))
            link(dve.tensor_scalar(mean[:, :], mean[:, :], 0.5, None, ALU.mult))
            link(dve.tensor_scalar(var[:, :], var[:, :], 1.0 / D, None, ALU.mult))
            dve.scalar_tensor_tensor(var[:, :], half_gap[:, :], 0.25, var[:, :], ALU.mult, ALU.add)\
                .then_inc(var_done, 1)
            dve.wait_ge(std_done, 1)
            link(dve.reciprocal(rstd[:, :], std[:, :]))
            with dve.Fori(0, NG // 2) as i:
                for s in range(2):
                    dve.wait_ge(xn_out[s], i * 16)
                    dve.wait_ge(t_done[s], i * KD)
                    for j in range(G):
                        t = (i * 2 + s) * G + j
                        col = lambda a: a[:, bass.ds(t, 1)]
                        dve.tensor_scalar(xnb[:, s, j:j + 1, :], xin[:, bass.ds(t, 1), :], col(mean), col(rstd),
                                          ALU.subtract, ALU.mult).then_inc(xn_done[s], 1)
            dve.wait_ge(hi_done, 2)
            dve.tensor_tensor(m.wqkv_l[:, :, :], raw_qkv[:, :, :], m.wqkv_h[:, :, :].bitcast(fp32), ALU.subtract)
            dve.tensor_tensor(m.wout_l[:, :, :], raw_out[:, :, :], m.wout_h[:, :, :].bitcast(fp32), ALU.subtract)
            dve.wait_ge(b1_t, 1)
            dve.tensor_copy(m.b1T[:, :], psB[:, 0:E * HC])
            for s in range(2):
                dve.wait_ge(xT_used[s], NG // 2)
            dve.tensor_copy(m.logits[:, :, :], psL[:, 0:NT * E].rearrange("p (t e) -> p t e", t=NT))

        @block.scalar
        def _(act):
            act.dma_start(wgs[:, :, :], wg.rearrange("(k p) e -> p k e", p=P)).then_inc(w_in, 16)
            act.dma_start(raw_b1[:, :], b1.rearrange("e (c p) -> (e c) p", p=P)).then_inc(w_in, 16)
            act.dma_start(raw_qkv[:, :, :], w_qkv.rearrange("(k p) n -> p k n", p=P)).then_inc(w_in, 16)
            for e in range(E):
                act.dma_start(m.b2b[:, e, :], b2[e:e + 1, :].broadcast_to([P, D])).then_inc(w_in, 16)
            act.wait_ge(wo_zero, 1)
            for h in range(NH):
                q, j = h // 4, h % 4
                act.dma_start(raw_out[32 * j:32 * j + DH, q, :], w_out[h * DH:(h + 1) * DH, :]).then_inc(w_in, 16)
            act.wait_ge(consts, 2)
            act.wait_ge(var_done, 1)
            act.activation(std[:, :], var[:, :], ACT.Sqrt, bias=eps[:, 0:1]).then_inc(std_done, 1)
            with act.Fori(0, NG // 2) as i:
                for s in range(2):
                    act.wait_ge(xT_used[s], i)
                    for k in range(KD):
                        act.wait_ge(t_done[s], KD * i + k + 1)
                        act.activation(xT[:, s, k, :], psT[2 * s + k][:, :], ACT.Copy).then_inc(xT_done[s], 1)
            act.wait_ge(w_in, 16 * (3 + E + NH))
            act.activation(m.wqkv_h[:, :, :], raw_qkv[:, :, :], ACT.Copy).then_inc(hi_done, 1)
            act.activation(m.wout_h[:, :, :], raw_out[:, :, :], ACT.Copy).then_inc(hi_done, 1)

        @block.tensor
        def _(pe):
            pe.wait_ge(consts, 2)
            pe.wait_ge(w_in, 16 * (3 + E + NH))
            pe.transpose(psB[:, 0:E * HC], raw_b1[:, :], m.eye[0:E * HC, 0:E * HC]).then_inc(b1_t, 1)
            with pe.Fori(0, NG // 2) as i:
                for s in range(2):
                    pe.wait_ge(xn_done[s], G * (i + 1))
                    pe.wait_ge(xT_done[s], i * KD)
                    for k in range(KD):
                        for j in range(G):
                            last = pe.transpose(psT[2 * s + k][:, j * P:(j + 1) * P],
                                                xnb[:, s, j, k * P:(k + 1) * P], m.eye[:, :])
                        last.then_inc(t_done[s], 1)
                    pe.wait_ge(xT_done[s], KD * (i + 1))
                    for j in range(G):
                        for k in range(KD):
                            last = pe.matmul(psL[:, bass.ds(((i * 2 + s) * G + j) * E, E)],
                                             xT[:, s, k, j * P:(j + 1) * P],
                                             wgs[:, k, :], start=(k == 0), stop=(k == KD - 1))
                    last.then_inc(xT_used[s], 1)


def route_phase(nc, m):
    C = K * NT
    ctx = ExitStack()
    with ctx:
        sb = lambda n, s, d: ctx.enter_context(nc.sbuf_tensor(n, s, d))
        sem = lambda n: ctx.enter_context(nc.semaphore(n))
        ps = lambda n: ctx.enter_context(nc.psum_tensor(n, [P, 512], fp32))
        t8 = lambda n: sb(n, [P, NT, E], fp32)
        tc = lambda n, d=fp32: sb(n, [P, C], d)
        shifted, ex, score, tmp, tmp2, oh = t8("r_sh"), t8("r_ex"), t8("r_sc"), t8("r_t"), t8("r_t2"), t8("r_oh")
        red = sb("r_red", [P, NT], fp32)
        topv = sb("r_topv", [P, K, NT], fp32)
        den = sb("r_den", [P, NT], fp32)
        OH = sb("r_OH", [P, E, C], fp32)
        OHb = sb("r_OHb", [P, E, C], bf16)
        cum = sb("r_cum", [P, E, C], fp32)
        pos8 = sb("r_pos8", [P, E, C], fp32)
        ones_c = tc("r_ones")
        eid, pos, valid, kept, slotf, dslot = tc("r_eid"), tc("r_pos"), tc("r_valid"), tc("r_kept"), tc("r_slotf"), tc("r_ds")
        dint, aint, bint = tc("r_di", i32), tc("r_ai", i32), tc("r_bi", i32)
        af, bf = tc("r_af"), tc("r_bf")
        tri = sb("r_tri", [P, P], bf16)
        ones = sb("r_onesb", [P, P], bf16)
        zeros = sb("r_zeros", [P, P], bf16)
        iota_e = sb("r_iota_e", [P, E], fp32)
        iota_e8 = sb("r_iota_e8", [P, E], fp32)
        iota_p = sb("r_iota_p", [P, 1], fp32)
        iota_t = sb("r_iota_t", [P, K, NT], fp32)
        iota_b = sb("r_iota_b", [P, P], bf16)
        R = 4
        ohB = sb("r_ohB", [P, R, P], bf16)
        ohA = sb("r_ohA", [P, R, 2, E * ST], bf16)
        tabp = sb("r_tabp", [P, E * ST], fp32)
        pre_ps, tot_ps, tab_ps = ps("r_pre"), ps("r_tot"), ps("r_tab")
        consts = sem("r_consts")
        chain = sem("r_chain")
        sh_done = sem("r_sh_done")
        ex_done = sem("r_ex_done")
        oh_done = sem("r_oh_done")
        sums_done = sem("r_sums")
        hot_ready = sem("r_hot")
        hot_used = sem("r_hot_used")
        tab_done = sem("r_tab_done")
        block = ctx.enter_context(nc.Block())

        @block.gpsimd
        def _(pool):
            pool.memset(zeros[:, :], 0.0).then_inc(consts, 1)
            pool.memset(ones[:, :], 1.0).then_inc(consts, 1)
            pool.memset(ones_c[:, :], 1.0).then_inc(consts, 1)
            pool.wait_ge(consts, 3)
            pool.affine_select(out=tri[:, :], in_=ones[:, :], compare_op=ALU.is_gt, fill=0.0, base=0,
                               pattern=[[1, P]], channel_multiplier=-1).then_inc(consts, 1)
            it = dict(allow_small_or_imprecise_dtypes=True)
            pool.iota(iota_e[:, :], pattern=[[1, E]], base=0, channel_multiplier=0, **it).then_inc(consts, 1)
            pool.iota(iota_e8[:, :], pattern=[[1, E]], base=-E, channel_multiplier=0, **it).then_inc(consts, 1)
            pool.iota(iota_p[:, :], pattern=[[1, 1]], base=0, channel_multiplier=1, **it).then_inc(consts, 1)
            pool.iota(iota_t[:, :, :], pattern=[[0, K], [1, NT]], base=0, channel_multiplier=0, **it).then_inc(consts, 1)
            pool.iota(iota_b[:, :], pattern=[[1, P]], base=0, channel_multiplier=0, **it).then_inc(consts, 1)

        @block.scalar
        def _(act):
            act.wait_ge(sh_done, 1)
            act.activation(ex[:, :, :], shifted[:, :, :], ACT.Exp).then_inc(ex_done, 1)

        @block.tensor
        def _(pe):
            pe.wait_ge(consts, 9)
            pe.wait_ge(oh_done, 1)
            flat = OHb[:, :, :].rearrange("p e c -> p (e c)")
            pe.matmul(pre_ps[:, :], tri[:, :], flat, start=True, stop=True)
            pe.matmul(tot_ps[:, :], ones[:, :], flat, start=True, stop=True).then_inc(sums_done, 1)
            hot = lambda r: ohA[:, r, :, :].rearrange("p a c -> p (a c)")
            pe.matmul(tab_ps[:, 0:2 * E * ST], zeros[:, :], zeros[:, :], start=True, stop=False)
            with pe.Fori(0, C // R) as i:
                for r in range(R):
                    pe.wait_ge(hot_ready, 3 * (i * R + r + 1))
                    pe.matmul(tab_ps[:, 0:2 * E * ST], ohB[:, r, :], hot(r), start=False, stop=False)\
                        .then_inc(hot_used, 1)
            pe.matmul(tab_ps[:, 0:2 * E * ST], zeros[:, :], zeros[:, :], start=False, stop=True).then_inc(tab_done, 1)

        @block.vector
        def _(dve):
            count = [0]

            def link(ins):
                count[0] += 1
                ins.then_inc(chain, 1)
                dve.wait_ge(chain, count[0])

            tokb = lambda t: t.unsqueeze(2).broadcast_to([P, NT, E])
            expb = lambda t: t.unsqueeze(1).broadcast_to([P, NT, E])
            link(dve.tensor_reduce(red[:, :], m.logits[:, :, :], AX.X, ALU.max))
            dve.tensor_tensor(shifted[:, :, :], m.logits[:, :, :], tokb(red[:, :]), ALU.subtract).then_inc(sh_done, 1)
            dve.wait_ge(ex_done, 1)
            link(dve.tensor_reduce(red[:, :], ex[:, :, :], AX.X, ALU.add))
            link(dve.reciprocal(red[:, :], red[:, :]))
            link(dve.tensor_tensor(score[:, :, :], ex[:, :, :], tokb(red[:, :]), ALU.mult))
            dve.wait_ge(consts, 9)
            for k in range(K):
                link(dve.tensor_reduce(topv[:, k, :], score[:, :, :], AX.X, ALU.max))
                link(dve.tensor_tensor(tmp[:, :, :], score[:, :, :], tokb(topv[:, k, :]), ALU.is_equal))
                link(dve.tensor_tensor(tmp2[:, :, :], tmp[:, :, :], expb(iota_e8[:, :]), ALU.mult))
                link(dve.tensor_reduce(red[:, :], tmp2[:, :, :], AX.X, ALU.min))
                link(dve.tensor_tensor(oh[:, :, :], expb(iota_e8[:, :]), tokb(red[:, :]), ALU.is_equal))
                link(dve.tensor_copy(OH[:, :, k * NT:(k + 1) * NT].rearrange("p e t -> p t e"), oh[:, :, :]))
                if k == 0:
                    link(dve.scalar_tensor_tensor(score[:, :, :], oh[:, :, :], -4.0, score[:, :, :],
                                                  ALU.mult, ALU.add))
            dve.tensor_copy(OHb[:, :, :], OH[:, :, :]).then_inc(oh_done, 1)
            link(dve.tensor_tensor(den[:, :], topv[:, 0, :], topv[:, 1, :], ALU.add))
            link(dve.reciprocal(den[:, :], den[:, :]))
            link(dve.tensor_tensor(topv[:, :, :], topv[:, :, :], den[:, :].unsqueeze(1).broadcast_to([P, K, NT]),
                                   ALU.mult))
            dve.wait_ge(sums_done, 1)
            tot = tot_ps[:, :].rearrange("p (e c) -> p e c", e=E)
            for e in range(E):
                link(dve.tensor_tensor_scan(cum[:, e, :], ones_c[:, :], tot[:, e, :], 0.0, ALU.mult, ALU.add))
            link(dve.tensor_tensor(pos8[:, :, :], cum[:, :, :], tot, ALU.subtract))
            link(dve.tensor_tensor(cum[:, :, :], pos8[:, :, :],
                                   pre_ps[:, :].rearrange("p (e c) -> p e c", e=E), ALU.add))
            link(dve.tensor_tensor(pos8[:, :, :], cum[:, :, :], OH[:, :, :], ALU.mult))
            link(dve.tensor_reduce(pos[:, :], pos8[:, :, :].rearrange("p e c -> p c e"), AX.X, ALU.add))
            link(dve.tensor_tensor(cum[:, :, :], OH[:, :, :],
                                   iota_e[:, :].unsqueeze(2).broadcast_to([P, E, C]), ALU.mult))
            link(dve.tensor_reduce(eid[:, :], cum[:, :, :].rearrange("p e c -> p c e"), AX.X, ALU.add))
            link(dve.tensor_scalar(valid[:, :], pos[:, :], float(CAP), None, ALU.is_lt))
            link(dve.tensor_tensor(m.gates[:, :], topv[:, :, :].rearrange("p k t -> p (k t)"), valid[:, :], ALU.mult))
            link(dve.tensor_tensor(kept[:, :], pos[:, :], valid[:, :], ALU.mult))
            link(dve.scalar_tensor_tensor(slotf[:, :], eid[:, :], float(CAP), kept[:, :], ALU.mult, ALU.add))
            link(dve.tensor_copy(m.slots[:, :], slotf[:, :]))
            link(dve.tensor_scalar(valid[:, :], valid[:, :], -2.0 * E * CAP, 2.0 * E * CAP, ALU.mult, ALU.add))
            link(dve.tensor_tensor(dslot[:, :], slotf[:, :], valid[:, :], ALU.add))
            link(dve.tensor_copy(dint[:, :], dslot[:, :]))
            link(dve.tensor_single_scalar(aint[:, :], dint[:, :], 7, ALU.arith_shift_right))
            link(dve.tensor_single_scalar(bint[:, :], dint[:, :], P - 1, ALU.bitwise_and))
            link(dve.tensor_copy(af[:, :], aint[:, :]))
            link(dve.tensor_copy(bf[:, :], bint[:, :]))
            tcol = iota_t[:, :, :].rearrange("p k t -> p (k t)")

            def one_hots(c, r):
                col = lambda t: t[:, bass.ds(c, 1)]
                dve.tensor_scalar(ohB[:, r, :], iota_b[:, :], col(bf), None, ALU.is_equal).then_inc(hot_ready, 1)
                dve.tensor_scalar(ohA[:, r, 0, :], iota_b[:, 0:E * ST], col(af), col(tcol),
                                  ALU.is_equal, ALU.mult).then_inc(hot_ready, 1)
                dve.tensor_scalar(ohA[:, r, 1, :], iota_b[:, 0:E * ST], col(af), iota_p[:, 0:1],
                                  ALU.is_equal, ALU.mult).then_inc(hot_ready, 1)

            for r in range(R):
                one_hots(r, r)
            with dve.Fori(1, C // R) as i:
                for r in range(R):
                    dve.wait_ge(hot_used, i * R + r - R + 1)
                    one_hots(i * R + r, r)
            dve.wait_ge(tab_done, 1)
            link(dve.tensor_copy(tabp[:, :], tab_ps[:, E * ST:2 * E * ST]))
            link(dve.scalar_tensor_tensor(m.token_of[:, :], tab_ps[:, 0:E * ST], float(P), tabp[:, :],
                                          ALU.mult, ALU.add))


def moe_phase(nc, m, xn_dram, w1, w2, y_dram):
    YR, FR = 4, 4
    ctx = ExitStack()
    with ctx:
        sb = lambda n, s, d: ctx.enter_context(nc.sbuf_tensor(n, s, d))
        sem = lambda n: ctx.enter_context(nc.semaphore(n))
        ps = lambda n: ctx.enter_context(nc.psum_tensor(n, [P, 512], fp32))
        raw1 = sb("m_raw1", [P, KD, H], fp32)
        raw2 = sb("m_raw2", [P, HC, D], fp32)
        w1h, w1l = sb("m_w1h", [P, KD, H], fp32r), sb("m_w1l", [P, KD, H], fp32r)
        w2h, w2l = sb("m_w2h", [P, HC, D], fp32r), sb("m_w2l", [P, HC, D], fp32r)
        idx = sb("m_idx", [P, ST], u32)
        xg = [sb(f"m_xg{j}", [P, D], fp32) for j in range(ST)]
        xh, xl = sb("m_xh", [P, KD, CAP], fp32r), sb("m_xl", [P, KD, CAP], fp32r)
        hf = sb("m_hf", [P, FR, HALF], fp32)
        hh, hl = sb("m_hh", [P, 2, HC, HALF], fp32r), sb("m_hl", [P, 2, HC, HALF], fp32r)
        yb = sb("m_y", [P, YR, D], fp32)
        psF = [ps(f"m_psF{i}") for i in range(4)]
        psY = [ps(f"m_psY{i}") for i in range(2)]
        psT = [ps(f"m_psT{i}") for i in range(2)]
        raw1_in, raw2_in = sem("m_raw1_in"), sem("m_raw2_in")
        w1h_done, w1l_done, w2h_done, w2l_done = (sem(f"m_{n}") for n in ("w1h_d", "w1l_d", "w2h_d", "w2l_d"))
        idx_done = sem("m_idx_done")
        xg_in = [sem(f"m_xg_in{j}") for j in range(ST)]
        t_done = sem("m_t_done")
        xh_done, xl_done = sem("m_xh_done"), sem("m_xl_done")
        f_done = sem("m_f_done")
        hh_done, hl_done = sem("m_hh_done"), sem("m_hl_done")
        y_done = sem("m_y_done")
        yb_done = sem("m_yb_done")
        y_out = [sem(f"m_y_out{i}") for i in range(YR)]
        U = 2 * HC
        TG = 2 * KD
        w1v = w1.rearrange("e (k p) h -> p (e k) h", p=P)
        w2v = w2.rearrange("e (c p) d -> p (e c) d", p=P)
        yv = y_dram.rearrange("(s p) d -> p s d", p=P)
        block = ctx.enter_context(nc.Block())

        def experts(eng, body):
            with eng.Fori(0, E - 1) as e:
                body(e, False)
            body(E - 1, True)

        @block.sync
        def _(sp):
            sp.dma_start(raw1[:, :, :], w1v[:, 0:KD, :]).then_inc(raw1_in, 16)
            sp.dma_start(raw2[:, :, :], w2v[:, 0:HC, :]).then_inc(raw2_in, 16)

            def body(e, last):
                if not last:
                    alone(sp, w1h_done, e + 1)
                    alone(sp, w1l_done, e + 1)
                    sp.dma_start(raw1[:, :, :], w1v[:, bass.ds((e + 1) * KD, KD), :]).then_inc(raw1_in, 16)
                    alone(sp, w2h_done, e + 1)
                    alone(sp, w2l_done, e + 1)
                    sp.dma_start(raw2[:, :, :], w2v[:, bass.ds((e + 1) * HC, HC), :]).then_inc(raw2_in, 16)
                for s in range(ST):
                    alone(sp, yb_done, e * ST + s + 3)
                    sp.dma_start(yv[:, bass.ds(e * ST + s, 1), :], yb[:, s % YR:s % YR + 1, :]).then_inc(y_out[s % YR], 16)
            experts(sp, body)
            for r in range(YR):
                sp.wait_ge(y_out[r], 16 * E * ST // YR)

        @block.gpsimd
        def _(pool):
            def gathers(e, first):
                if not first:
                    alone(pool, t_done, e * TG)
                pool.tensor_copy(idx[:, :], m.token_of[:, bass.ds(e * ST, ST)]).then_inc(idx_done, 1)
                alone(pool, idx_done, e + 1)
                for j in range(ST):
                    pool.indirect_dma_start(xg[j][:, :], None, xn_dram,
                                            bass.IndirectOffsetOnAxis(ap=idx[:, j:j + 1], axis=0))\
                        .then_inc(xg_in[j], 16)
            gathers(0, True)
            with pool.Fori(1, E) as e:
                gathers(e, False)

        @block.scalar
        def _(act):
            def w1_high(e):
                act.wait_ge(raw1_in, (e + 1) * 16)
                act.activation(w1h[:, :, :], raw1[:, :, :], ACT.Copy).then_inc(w1h_done, 1)

            def x_high(e):
                for g in range(TG):
                    act.wait_ge(t_done, e * TG + g + 1)
                    act.activation(xh[:, g % KD, (g // KD) * HALF:(g // KD + 1) * HALF], psT[g % 2][:, :], ACT.Copy)\
                        .then_inc(xh_done, 1)

            w1_high(0)
            x_high(0)

            def body(e, last):
                for u in range(U):
                    if u == 4:
                        act.wait_ge(y_done, e * ST)
                        act.wait_ge(raw2_in, (e + 1) * 16)
                        act.activation(w2h[:, :, :], raw2[:, :, :], ACT.Copy).then_inc(w2h_done, 1)
                    act.wait_ge(f_done, e * U + u + 1)
                    alone(act, hl_done, e * U + u + 1)
                    bias = m.b1T[:, bass.ds(e * HC + u % HC, 1)]
                    act.activation(hf[:, u % FR, :], psF[u % 4][:, :], ACT.Relu, bias=bias)
                    if u == 0:
                        alone(act, y_done, e * ST)
                    act.activation(hh[:, u // HC, u % HC, :], psF[u % 4][:, :], ACT.Relu, bias=bias)\
                        .then_inc(hh_done, 1)
                if not last:
                    w1_high(e + 1)
                    x_high(e + 1)
            experts(act, body)

        @block.vector
        def _(dve):
            def w1_low(e):
                dve.wait_ge(w1h_done, e + 1)
                dve.tensor_tensor(w1l[:, :, :], raw1[:, :, :], w1h[:, :, :].bitcast(fp32), ALU.subtract)\
                    .then_inc(w1l_done, 1)

            def x_low(e):
                for g in range(TG):
                    k, half = g % KD, g // KD
                    dve.wait_ge(xh_done, e * TG + g + 1)
                    dve.tensor_tensor(xl[:, k, half * HALF:(half + 1) * HALF], psT[g % 2][:, :],
                                      xh[:, k, half * HALF:(half + 1) * HALF].bitcast(fp32), ALU.subtract)\
                        .then_inc(xl_done, 1)

            def y_row(e, s):
                dve.wait_ge(y_done, e * ST + s + 1)
                if s >= YR:
                    dve.wait_ge(y_out[s % YR], 16 * (2 * e + 1))
                else:
                    dve.wait_ge(y_out[s % YR], 32 * e)
                dve.tensor_tensor(yb[:, s % YR:s % YR + 1, :], psY[s % 2][:, 0:D].unsqueeze(1),
                                  m.b2b[:, bass.ds(e, 1), :], ALU.add).then_inc(yb_done, 1)

            dve.sem_inc(hl_done, FR)
            dve.sem_inc(yb_done, 2)
            w1_low(0)
            x_low(0)

            def body(e, last):
                for u in range(U):
                    if u == 4:
                        dve.wait_ge(w2h_done, e + 1)
                        dve.tensor_tensor(w2l[:, :, :], raw2[:, :, :], w2h[:, :, :].bitcast(fp32), ALU.subtract)\
                            .then_inc(w2l_done, 1)
                    dve.wait_ge(hh_done, e * U + u + 1)
                    dve.tensor_tensor(hl[:, u // HC, u % HC, :], hf[:, u % FR, :],
                                      hh[:, u // HC, u % HC, :].bitcast(fp32), ALU.subtract).then_inc(hl_done, 1)
                if not last:
                    w1_low(e + 1)
                for s in range(ST):
                    if s == ST // 2 and not last:
                        x_low(e + 1)
                    y_row(e, s)
            experts(dve, body)

        @block.tensor
        def _(pe):
            def transposes(e):
                for g in range(TG):
                    k, half = g % KD, g // KD
                    pe.wait_ge(xl_done, e * TG + g + 1)
                    for j in range(ST // 2):
                        if k == 0:
                            pe.wait_ge(xg_in[half * ST // 2 + j], (e + 1) * 16)
                        last = pe.transpose(psT[g % 2][:, j * P:(j + 1) * P],
                                            xg[half * ST // 2 + j][:, k * P:(k + 1) * P], m.eye[:, :])
                    last.then_inc(t_done, 1)

            pe.sem_inc(xl_done, 2)
            transposes(0)

            def body(e, last):
                pe.wait_ge(w1h_done, e + 1)
                pe.wait_ge(w1l_done, e + 1)
                for u in range(U):
                    half, c = u // HC, u % HC
                    if c == 0:
                        pe.wait_ge(xl_done, e * TG + 2 + KD * (half + 1))
                    pe.wait_ge(hl_done, e * U + u + 1)
                    cols = slice(half * HALF, (half + 1) * HALF)
                    split_products(pe, psF[u % 4][:, :],
                                   [(w1h[:, k, c * P:(c + 1) * P], w1l[:, k, c * P:(c + 1) * P],
                                     xh[:, k, cols], xl[:, k, cols]) for k in range(KD)]).then_inc(f_done, 1)
                pe.wait_ge(w2h_done, e + 1)
                pe.wait_ge(w2l_done, e + 1)
                for s in range(ST):
                    half, j = s // (ST // 2), s % (ST // 2)
                    if s == ST // 2 and not last:
                        transposes(e + 1)
                    if j == 0:
                        pe.wait_ge(hl_done, e * U + FR + HC * (half + 1))
                    pe.wait_ge(yb_done, e * ST + s + 1)
                    split_products(pe, psY[s % 2][:, 0:D],
                                   [(hh[:, half, c, j * P:(j + 1) * P], hl[:, half, c, j * P:(j + 1) * P],
                                     w2h[:, c, :], w2l[:, c, :]) for c in range(HC)]).then_inc(y_done, 1)
            experts(pe, body)


def attention_phase(nc, m, x, xn_dram, y_dram, out):
    BLK = 2
    NGR = QUADS * NB // BLK
    LAG_T, LAG_C, LAG_V, LAG_O = 3, 4, 5, 6
    TT = L // P
    PAD = WIN
    KW = PAD + L + 2 * WIN
    USES = 2 * KD + 8 + NB + TT
    ctx = ExitStack()
    with ctx:
        sb = lambda n, s, d: ctx.enter_context(nc.sbuf_tensor(n, s, d))
        sem = lambda n: ctx.enter_context(nc.semaphore(n))
        ps = lambda n: ctx.enter_context(nc.psum_tensor(n, [P, 512], fp32))
        two = lambda n: [sem(f"{n}{i}") for i in range(2)]
        four = lambda n: [sem(f"{n}{i}") for i in range(4)]
        xnr = sb("a_xn", [P, TT, D], fp32)
        xTh, xTl = sb("a_xTh", [P, KD, PAD + L], fp32r), sb("a_xTl", [P, KD, PAD + L], fp32r)
        qkh, qkl = sb("a_qkh", [P, 4, L], fp32r), sb("a_qkl", [P, 4, L], fp32r)
        v = sb("a_v", [P, NB, D], fp32)
        qs = [sb(f"a_qs{i}", [P, NB, 2, WIN], fp32r) for i in range(4)]
        ks = [sb(f"a_ks{i}", [P, KW], fp32r) for i in range(4)]
        pr = sb("a_p", [P, 4, BLK, 2, P], fp32)
        nmax = sb("a_nmax", [P, 4, 2 * BLK], fp32)
        sums = sb("a_sums", [P, 4, 2 * BLK], fp32)
        rsum = sb("a_rsum", [P, 4, 2 * BLK], fp32)
        pT = sb("a_pT", [P, 2, 2 * BLK, P], fp32)
        oTh, oTl = sb("a_oTh", [P, QUADS, L], fp32r), sb("a_oTl", [P, QUADS, L], fp32r)
        res = sb("a_res", [P, TT, D], fp32)
        idx = sb("a_idx", [P, K, TT], u32)
        yg = [sb(f"a_yg{i}", [P, D], fp32) for i in range(4)]
        psA = [ps("a_psA0"), ps("a_psA1")]
        psS = [ps("a_psS0"), ps("a_psS1")]
        psP = [ps("a_psP0"), ps("a_psP1")]
        psO = [ps("a_psO0"), ps("a_psO1")]
        zeroed = sem("a_zeroed")
        xn_in = sem("a_xn_in")
        a_done, a_high, a_free = two("a_gen_done"), two("a_gen_high"), two("a_gen_free")
        stack_in = four("a_stack_in")
        s_done = two("a_s_done")
        max_done, exp_done, rsum_done, norm_done = (sem(f"a_{n}") for n in ("max", "exp", "rsum", "norm"))
        t_done, pT_done, pT_used = two("a_t_done"), two("a_pT_done"), two("a_pT_used")
        o_high, o_free = two("a_o_high"), two("a_o_free")
        res_in, res_out = sem("a_res_in"), sem("a_res_out")
        idx_done = sem("a_idx_done")
        yg_in = four("a_yg_in")
        acc = sem("a_acc")
        xnv = xn_dram.rearrange("(t p) d -> p t d", p=P)
        xv = x.rearrange("b (t p) d -> p (b t) d", p=P)
        ov = out.rearrange("b (t p) d -> p (b t) d", p=P)
        block = ctx.enter_context(nc.Block())
        T0, Q0, V0, O0 = 0, 2 * KD, 2 * KD + 8, 2 * KD + 8 + NB

        def used(b, n):
            return b * (USES // 2) + n // 2

        @block.sync
        def _(sp):
            with sp.Fori(0, B) as b:
                sp.dma_start(xnr[:, :, :], xnv[:, bass.ds(b * TT, TT), :]).then_inc(xn_in, 16)
                alone(sp, res_out, b * 32)
                sp.dma_start(res[:, :, :], xv[:, bass.ds(b * TT, TT), :]).then_inc(res_in, 16)
                sp.wait_ge(zeroed, 3)
                for q in range(QUADS):
                    mt = q // 2
                    for i in range(2):
                        alone(sp, a_free[i], used(b, Q0 + 4 * (mt + 1)))
                        if q >= 2:
                            alone(sp, s_done[i], b * (NGR * BLK // 2) + (q - 1) * NB // 2)
                    for a in range(2):
                        slot = (2 * q + a) % 4
                        for s in range(2):
                            h = 4 * q + 2 * a + s
                            src = slice(DH * (h % 8), DH * (h % 8) + DH)
                            for r in range(4):
                                row = slice(64 * s + DH * r, 64 * s + DH * (r + 1))
                                sp.dma_start(qs[slot][row, :, s, :].bitcast(fp32),
                                             (qkh if r < 2 else qkl)[src, mt, :].bitcast(fp32)
                                             .rearrange("p (n t) -> p n t", n=NB))\
                                    .then_inc(stack_in[slot], 16)
                                sp.dma_start(ks[slot][row, PAD:PAD + L].bitcast(fp32),
                                             (qkl if r % 2 else qkh)[src, 2 + mt, :].bitcast(fp32))\
                                    .then_inc(stack_in[slot], 16)
                for half in range(2):
                    for i in range(2):
                        alone(sp, a_free[i], used(b, O0 + (half + 1) * TT // 2))
                    sp.dma_start(ov[:, bass.ds(b * TT + half * TT // 2, TT // 2), :],
                                 res[:, half * TT // 2:(half + 1) * TT // 2, :]).then_inc(res_out, 16)
            sp.wait_ge(res_out, B * 32)

        @block.gpsimd
        def _(pool):
            for i in range(4):
                z = pool.memset(ks[i][:, 0:PAD].bitcast(fp32), 0.0)
                z = pool.memset(ks[i][:, PAD + L:KW].bitcast(fp32), 0.0)
            z.then_inc(zeroed, 1)
            with pool.Fori(0, B) as b:
                slots = m.slots[:, :].rearrange("p (k t) -> p k t", k=K)
                alone(pool, acc, b * TT * K)
                pool.tensor_copy(idx[:, :, :], slots[:, :, bass.ds(b * TT, TT)]).then_inc(idx_done, 1)
                alone(pool, idx_done, b + 1)
                for g in range(NGR):
                    alone(pool, rsum_done, b * NGR + g + 1)
                    r = g % 4
                    for c in range(2 * BLK):
                        e = pr[:, r, c // 2, c % 2, :]
                        pool.tensor_scalar(e, e, rsum[:, r, c:c + 1], 0.0, ALU.mult, ALU.add).then_inc(norm_done, 1)
                    if g % 2 == 0:
                        i = g // 2
                        if i >= 4:
                            alone(pool, acc, b * TT * K + i - 3)
                        pool.indirect_dma_start(yg[i % 4][:, :], None, y_dram,
                                                bass.IndirectOffsetOnAxis(ap=idx[:, i % 2, i // 2:i // 2 + 1], axis=0))\
                            .then_inc(yg_in[i % 4], 16)

        @block.scalar
        def _(act):
            with act.Fori(0, B) as b:
                for g in range(2):
                    for k in range(KD):
                        n = T0 + g * KD + k
                        act.wait_ge(a_done[n % 2], used(b, n) + 1)
                        act.activation(xTh[:, k, PAD + g * 512:PAD + (g + 1) * 512], psA[n % 2][:, :], ACT.Copy)\
                            .then_inc(a_high[n % 2], 1)
                for i in range(8):
                    n = Q0 + i
                    mt, c = (0, 2, 1, 3)[i // 2], i % 2
                    act.wait_ge(a_done[n % 2], used(b, n) + 1)
                    act.activation(qkh[:, mt, c * 512:(c + 1) * 512], psA[n % 2][:, :], ACT.Copy)\
                        .then_inc(a_high[n % 2], 1)
                for w in range(NB):
                    n = V0 + w
                    act.wait_ge(a_done[n % 2], used(b, n) + 1)
                    act.activation(v[:, w, :], psA[n % 2][:, 0:D], ACT.Copy).then_inc(a_free[n % 2], 1)
                for step in range(NGR + LAG_O):
                    g = step
                    if g < NGR:
                        r = g % 4
                        for c in range(2 * BLK):
                            act.wait_ge(max_done, (b * NGR + g) * 2 * BLK + c + 1)
                            e = pr[:, r, c // 2, c % 2, :]
                            act.activation(e, e, ACT.Exp, scale=-1.0, bias=nmax[:, r, c:c + 1],
                                           accum_out=sums[:, r, c:c + 1]).then_inc(exp_done, 1)
                    g = step - LAG_O
                    if g >= 0 and g % 4 == 3:
                        q, half = g // 8, g // 4 % 2
                        act.wait_ge(pT_used[1], b * (NGR // 2) + g // 2 + 1)
                        act.activation(oTh[:, q, half * 512:(half + 1) * 512], psO[half][:, :], ACT.Copy)\
                            .then_inc(o_high[half], 1)

        @block.vector
        def _(dve):
            for t in (xTh, xTl):
                z = dve.memset(t[:, :, 0:PAD].bitcast(fp32), 0.0)
            z.then_inc(zeroed, 1)
            for t in psO:
                dve.memset(t[:, :], 0.0)
            for t in qs:
                dve.memset(t[0:64, :, 1, :].bitcast(fp32), 0.0)
                z = dve.memset(t[64:P, :, 0, :].bitcast(fp32), 0.0)
            z.then_inc(zeroed, 1)
            with dve.Fori(0, B) as b:
                for g in range(2):
                    for k in range(KD):
                        n = T0 + g * KD + k
                        cols = slice(PAD + g * 512, PAD + (g + 1) * 512)
                        dve.wait_ge(a_high[n % 2], b * 6 + n // 2 + 1)
                        dve.tensor_tensor(xTl[:, k, cols], psA[n % 2][:, :], xTh[:, k, cols].bitcast(fp32),
                                          ALU.subtract).then_inc(a_free[n % 2], 1)
                for i in range(8):
                    n = Q0 + i
                    mt, c = (0, 2, 1, 3)[i // 2], i % 2
                    cols = slice(c * 512, (c + 1) * 512)
                    dve.wait_ge(a_high[n % 2], b * 6 + n // 2 + 1)
                    dve.tensor_tensor(qkl[:, mt, cols], psA[n % 2][:, :], qkh[:, mt, cols].bitcast(fp32),
                                      ALU.subtract).then_inc(a_free[n % 2], 1)
                dve.wait_ge(res_in, (b + 1) * 16)
                for step in range(NGR + LAG_O):
                    g = step - LAG_C
                    if 0 <= g < NGR:
                        u = g % 2
                        dve.wait_ge(t_done[u], b * (NGR // 2) + g // 2 + 1)
                        dve.wait_ge(pT_used[u], b * (NGR // 2) + g // 2)
                        dve.tensor_copy(pT[:, u, :, :].rearrange("p c q -> p (c q)"), psP[u][:, :])\
                            .then_inc(pT_done[u], 1)
                    g = step
                    if g < NGR:
                        r = g % 4
                        if g >= 4:
                            dve.wait_ge(t_done[g % 2], b * (NGR // 2) + g // 2 - 1)
                        for j in range(BLK):
                            n = g * BLK + j
                            blk = n % NB
                            alone(dve, s_done[n % 2], b * (NGR * BLK // 2) + n // 2 + 1)
                            for a in range(2):
                                c = 2 * j + a
                                ins = dve.tensor_tensor_reduce(
                                    out=pr[:, r, j, a, :], in0=psS[n % 2][:, a * 256:a * 256 + P],
                                    in1=m.mask[:, 1 if blk == 0 else 0, :], scale=-(DH ** -0.5), scalar=BIG,
                                    op0=ALU.add, op1=ALU.min, accum_out=nmax[:, r, c:c + 1])
                                ins.then_inc(max_done, 1)
                    g = step - 1
                    if 0 <= g < NGR:
                        dve.wait_ge(exp_done, (b * NGR + g + 1) * 2 * BLK)
                        dve.reciprocal(rsum[:, g % 4, :], sums[:, g % 4, :]).then_inc(rsum_done, 1)
                    g = step - LAG_C
                    if 0 <= g < NGR and g % 2 == 1:
                        i = g // 2
                        t, k = i // 2, i % 2
                        dve.wait_ge(yg_in[i % 4], 16 * (b * 4 + i // 4 + 1))
                        if k == 1:
                            dve.wait_ge(acc, b * TT * K + i)
                        dve.scalar_tensor_tensor(res[:, t, :], yg[i % 4][:, :],
                                                 m.gates[:, bass.ds(b * TT + k * NT + t, 1)], res[:, t, :],
                                                 ALU.mult, ALU.add).then_inc(acc, 1)
                    g = step - LAG_O
                    if g >= 0 and g % 4 == 3:
                        q, half = g // 8, g // 4 % 2
                        cols = slice(half * 512, (half + 1) * 512)
                        dve.wait_ge(o_high[half], b * QUADS + q + 1)
                        dve.tensor_tensor(oTl[:, q, cols], psO[half][:, :], oTh[:, q, cols].bitcast(fp32),
                                          ALU.subtract).then_inc(o_free[half], 1)
                for t in range(TT):
                    n = O0 + t
                    dve.wait_ge(a_done[n % 2], used(b, n) + 1)
                    dve.wait_ge(acc, (b + 1) * TT * K)
                    dve.tensor_tensor(res[:, t, :], res[:, t, :], psA[n % 2][:, 0:D], ALU.add)\
                        .then_inc(a_free[n % 2], 1)

        @block.tensor
        def _(pe):
            pe.wait_ge(zeroed, 3)
            with pe.Fori(0, B) as b:
                pe.wait_ge(xn_in, (b + 1) * 16)
                for g in range(2):
                    for k in range(KD):
                        n = T0 + g * KD + k
                        pe.wait_ge(a_free[n % 2], used(b, n))
                        for j in range(4):
                            last = pe.transpose(psA[n % 2][:, j * P:(j + 1) * P],
                                                xnr[:, g * 4 + j, k * P:(k + 1) * P], m.eye[:, :])
                        last.then_inc(a_done[n % 2], 1)
                for i in range(8):
                    n = Q0 + i
                    mt, c = (0, 2, 1, 3)[i // 2], i % 2
                    if i == 0:
                        for u in range(2):
                            pe.wait_ge(a_free[u], used(b, Q0))
                    pe.wait_ge(a_free[n % 2], used(b, n))
                    w, cols = slice(mt * P, (mt + 1) * P), slice(PAD + c * 512, PAD + (c + 1) * 512)
                    split_products(pe, psA[n % 2][:, :],
                                   [(m.wqkv_h[:, k, w], m.wqkv_l[:, k, w], xTh[:, k, cols], xTl[:, k, cols])
                                    for k in range(KD)]).then_inc(a_done[n % 2], 1)
                for w in range(NB):
                    n = V0 + w
                    pe.wait_ge(a_free[n % 2], used(b, n))
                    cols, vc = slice(w * WIN, w * WIN + P), slice(2 * D, 3 * D)
                    split_products(pe, psA[n % 2][:, 0:D],
                                   [(xTh[:, k, cols], xTl[:, k, cols], m.wqkv_h[:, k, vc], m.wqkv_l[:, k, vc])
                                    for k in range(KD)]).then_inc(a_done[n % 2], 1)
                for step in range(NGR + LAG_V):
                    g = step
                    if g < NGR:
                        q = g // 8
                        if g % 8 == 0:
                            for a in range(2):
                                pe.wait_ge(stack_in[(2 * q + a) % 4], 256 * (b * 2 + q // 2 + 1))
                        for j in range(BLK):
                            n = g * BLK + j
                            blk = n % NB
                            if n >= 2:
                                pe.wait_ge(max_done, (b * NGR * BLK + n - 1) * 2)
                            for a in range(2):
                                slot = (2 * q + a) % 4
                                last = pe.matmul(psS[n % 2][:, a * 256:(a + 1) * 256],
                                                 qs[slot][:, blk, :, :].rearrange("p s t -> p (s t)"),
                                                 ks[slot][:, blk * WIN:blk * WIN + 256], start=True, stop=True)
                            last.then_inc(s_done[n % 2], 1)
                    g = step - LAG_T
                    if 0 <= g < NGR:
                        u = g % 2
                        pe.wait_ge(norm_done, (b * NGR + g + 1) * 2 * BLK)
                        pe.wait_ge(pT_done[u], b * (NGR // 2) + g // 2)
                        for c in range(2 * BLK):
                            last = pe.transpose(psP[u][:, c * P:(c + 1) * P], pr[:, g % 4, c // 2, c % 2, :],
                                                m.eye[:, :])
                        last.then_inc(t_done[u], 1)
                    g = step - LAG_V
                    if 0 <= g < NGR:
                        u, q, half = g % 2, g // 8, g // 4 % 2
                        if g == 0:
                            for i in range(2):
                                pe.wait_ge(a_free[i], used(b, O0))
                        pe.wait_ge(pT_done[u], b * (NGR // 2) + g // 2 + 1)
                        if g % 4 == 0:
                            pe.wait_ge(o_free[half], b * QUADS + q)
                        for j in range(BLK):
                            blk = (g * BLK + j) % NB
                            for c in range(4):
                                h = 4 * q + c
                                last = pe.matmul(psO[half][32 * c:32 * c + DH, (blk % 8) * WIN:(blk % 8 + 1) * WIN],
                                                 v[:, blk, h * DH:(h + 1) * DH],
                                                 pT[:, u, 2 * j + c // 2, (c % 2) * WIN:(c % 2 + 1) * WIN],
                                                 start=True, stop=True)
                        last.then_inc(pT_used[u], 1)
                for t in range(TT):
                    n = O0 + t
                    if t % 4 == 0:
                        pe.wait_ge(o_free[t // 4], (b + 1) * QUADS)
                    pe.wait_ge(a_free[n % 2], used(b, n))
                    cols = slice(t * P, (t + 1) * P)
                    split_products(pe, psA[n % 2][:, 0:D],
                                   [(oTh[:, q, cols], oTl[:, q, cols], m.wout_h[:, q, :], m.wout_l[:, q, :])
                                    for q in range(QUADS)]).then_inc(a_done[n % 2], 1)


def build(nc, x, w_qkv, w_out, wg, w1, b1, w2, b2, out):
    ctx = ExitStack()
    with ctx:
        sb = lambda n, s, d: ctx.enter_context(nc.sbuf_tensor(n, s, d))
        xn_dram = nc.dram_tensor("xn_scratch", (N, D), fp32, kind="Internal").ap()
        y_dram = nc.dram_tensor("y_scratch", (E * CAP, D), fp32, kind="Internal").ap()
        m = Mem()
        Mem.passed = ctx.enter_context(nc.semaphore("waits_passed"))
        m.eye = sb("eye", [P, P], fp32)
        m.mask = sb("mask", [P, 2, 2 * WIN], fp32)
        m.logits = sb("logits", [P, NT, E], fp32)
        m.wqkv_h, m.wqkv_l = sb("wqkv_h", [P, KD, 3 * D], fp32r), sb("wqkv_l", [P, KD, 3 * D], fp32r)
        m.wout_h, m.wout_l = sb("wout_h", [P, QUADS, D], fp32r), sb("wout_l", [P, QUADS, D], fp32r)
        m.gates = sb("gates", [P, K * NT], fp32)
        m.slots = sb("slots", [P, K * NT], u32)
        m.token_of = sb("token_of", [P, E * ST], u32)
        with ExitStack() as inner:
            m.b1T = inner.enter_context(nc.sbuf_tensor("b1T", [P, E * HC], fp32))
            m.b2b = inner.enter_context(nc.sbuf_tensor("b2b", [P, E, D], fp32))
            norm_phase(nc, m, x, xn_dram, wg, w_qkv, w_out, b1, b2)
            route_phase(nc, m)
            moe_phase(nc, m, xn_dram, w1, w2, y_dram)
        attention_phase(nc, m, x, xn_dram, y_dram, out)


_INS = ['L0_attn_x', 'L0_attn_w_qkv', 'L0_attn_w_out', 'L0_ffn_wg', 'L0_ffn_w1', 'L0_ffn_b1', 'L0_ffn_w2',
        'L0_ffn_b2']


def kernel(**inputs):
    import numpy as _np
    import concourse.bacc as _bacc
    from concourse import mybir as _mybir
    from concourse.bass_utils import run_bass_kernel_spmd as _run

    nc = _bacc.Bacc("TRN2", target_bir_lowering=False, num_devices=1)
    arrays, args = {}, []
    for name in _INS:
        a = _np.ascontiguousarray(inputs[name])
        arrays[f"in_{name}"] = a
        args.append(nc.dram_tensor(f"in_{name}", a.shape, _mybir.dt.from_np(a.dtype), kind="ExternalInput").ap())
    o = nc.dram_tensor("out_0", (B, L, D), fp32, kind="ExternalOutput").ap()
    build(nc, *args, o)
    r = _run(nc, [arrays], core_ids=[0])
    return r.results[0]["out_0"]
```

```python
import concourse.bass as bass
from concourse import mybir
from contextlib import ExitStack

fp32 = mybir.dt.float32
fp32r = mybir.dt.float32r
bf16 = mybir.dt.bfloat16
u32 = mybir.dt.uint32
i32 = mybir.dt.int32
ALU = mybir.AluOpType
ACT = mybir.ActivationFunctionType
AX = mybir.AxisListType

P = 128
B, L, D = 4, 1024, 256
N = B * L
KD = D // P
NT = N // P
E, K, H = 8, 2, 1024
CAP = K * N // E
HC = H // P
ST = CAP // P
HALF = CAP // 2
NH, DH, WIN = 16, 16, 64
NB = L // WIN
NEG = -1e30
EPS = 1e-5
BIG = 3e38


class Mem:
    pass


def alone(eng, sem, value):
    eng.wait_ge(sem, value)
    eng.sem_inc(Mem.passed, 1)


def split_products(pe, out, pairs, n_start=True, n_stop=True):
    last, n = None, 3 * len(pairs)
    i = 0
    for lh, ll, rh, rl in pairs:
        for a, b in ((lh, rh), (lh, rl), (ll, rh)):
            last = pe.matmul(out, a, b, start=(n_start and i == 0), stop=(n_stop and i == n - 1))
            i += 1
    return last


def norm_phase(nc, m, x, xn_dram, wg, w_qkv, w_out, b1, b2):
    G, C = 4, 4
    TURNS = NT // (G * C)
    ctx = ExitStack()
    with ctx:
        sb = lambda n, s, d: ctx.enter_context(nc.sbuf_tensor(n, s, d))
        sem = lambda n: ctx.enter_context(nc.semaphore(n))
        ps = lambda n: ctx.enter_context(nc.psum_tensor(n, [P, 512], fp32))
        each = lambda n: [sem(f"{n}{c}") for c in range(C)]
        xin = [sb(f"n_xin{c}", [P, G, D], fp32) for c in range(C)]
        xnb = [sb(f"n_xn{c}", [P, G, D], fp32) for c in range(C)]
        stats = sb("n_stats", [P, C, G, 6], fp32)
        total, gap, spread, gap2, mean, var, std, rstd = (
            sb(f"n_{n}", [P, C, G], fp32) for n in ("total", "gap", "spread", "gap2", "mean", "var", "std", "rstd"))
        eps = sb("n_eps", [P, 1], fp32)
        xT = sb("n_xT", [P, C, KD, G * P], fp32)
        lT = sb("n_lT", [P, G * P], fp32)
        wgs = sb("n_wg", [P, KD, E], fp32)
        raw_b1 = sb("n_rawb1", [E * HC, P], fp32)
        psT = [ps(f"n_psT{i}") for i in range(4)]
        psL, psX, psB = ps("n_psL"), ps("n_psX"), ps("n_psB")
        x_in, norm_done, xn_out = each("n_x_in"), each("n_norm_done"), each("n_xn_out")
        wg_in, w_in = sem("n_wg_in"), sem("n_w_in")
        consts, made, chain = sem("n_consts"), sem("n_made"), sem("n_chain")
        var_done, std_done, rstd_done = sem("n_var_done"), sem("n_std_done"), sem("n_rstd_done")
        t_done, xT_done = sem("n_t_done"), sem("n_xT_done")
        lT_done, lT_copied, l_done, l_copied = sem("n_lT_done"), sem("n_lT_copied"), sem("n_l_done"), sem("n_l_copied")
        b1_t = sem("n_b1_t")
        xv = x.rearrange("b (t p) d -> p (b t) d", p=P)
        xnv = xn_dram.rearrange("(t p) d -> p t d", p=P)
        block = ctx.enter_context(nc.Block())
        TD = KD * C

        def xn_free(eng, i, c):
            eng.wait_ge(xn_out[c], 16 * (i + 1))
            eng.wait_ge(t_done, i * TD + KD * (c + 1))

        def normalise(eng, c, tiles):
            for j in tiles:
                eng.tensor_scalar(xnb[c][:, j, :], xin[c][:, j, :], mean[:, c, j:j + 1], rstd[:, c, j:j + 1],
                                  ALU.subtract, ALU.mult).then_inc(norm_done[c], 1)

        @block.sync
        def _(sp):
            for c in range(C):
                sp.dma_start(xin[c][:, :, :], xv[:, c * G:(c + 1) * G, :]).then_inc(x_in[c], 16)
            for i in range(TURNS):
                for c in range(C):
                    sp.wait_ge(norm_done[c], G * (i + 1))
                    t = (i * C + c) * G
                    if i + 1 < TURNS:
                        sp.dma_start(xin[c][:, :, :], xv[:, t + C * G:t + (C + 1) * G, :]).then_inc(x_in[c], 16)
                    sp.dma_start(xnv[:, t:t + G, :], xnb[c][:, :, :]).then_inc(xn_out[c], 16)
            for c in range(C):
                sp.wait_ge(xn_out[c], 16 * (TURNS + 1))

        @block.gpsimd
        def _(pool):
            pool.memset(m.eye[:, :], 0.0).then_inc(made, 1)
            pool.wait_ge(made, 1)
            pool.affine_select(out=m.eye[:, :], in_=m.eye[:, :], compare_op=ALU.not_equal, fill=1.0,
                               base=0, pattern=[[-1, P]], channel_multiplier=1).then_inc(consts, 1)
            for c in range(C):
                pool.sem_inc(xn_out[c], 16)
            with pool.Fori(0, TURNS) as i:
                for c in range(C):
                    xn_free(pool, i, c)
                    alone(pool, rstd_done, i * C + c + 1)
                    normalise(pool, c, (G - 1,))
            pool.memset(m.mask[:, :, :], 0.0).then_inc(made, 1)
            n = 2
            for sign in (1, -1):
                pool.wait_ge(made, n)
                for first in range(2):
                    for s in range(2):
                        part = m.mask[s * WIN:(s + 1) * WIN, first, :]
                        pool.affine_select(out=part, in_=part, compare_op=ALU.is_ge, fill=NEG,
                                           base=-1 if sign == 1 else WIN, pattern=[[sign, 2 * WIN]],
                                           channel_multiplier=-sign).then_inc(made, 1)
                        n += 1
            pool.wait_ge(made, n)
            pool.memset(m.mask[:, 1, 0:WIN], NEG)

        @block.vector
        def _(dve):
            LINKS = 3 * C

            def link(ins, value):
                ins.then_inc(chain, 1)
                dve.wait_ge(chain, value)

            def statistics(i, c):
                dve.wait_ge(x_in[c], 16 * (i + 1))
                for j in range(G):
                    ins = dve.bn_stats(stats[:, c, j, :], xin[c][:, j, :])
                n = i * LINKS + 3 * c
                link(ins, n + 1)
                even = lambda k: stats[:, c, :, k]
                dve.tensor_tensor(total[:, c, :], even(1), even(4), ALU.add)
                dve.tensor_tensor(gap[:, c, :], even(1), even(4), ALU.subtract)
                link(dve.tensor_tensor(spread[:, c, :], even(2), even(5), ALU.add), n + 2)
                dve.tensor_scalar(mean[:, c, :], total[:, c, :], 0.5, None, ALU.mult)
                link(dve.scalar_tensor_tensor(gap2[:, c, :], gap[:, c, :], 0.25, gap[:, c, :], ALU.mult, ALU.mult),
                     n + 3)
                dve.scalar_tensor_tensor(var[:, c, :], spread[:, c, :], 1.0 / D, gap2[:, c, :], ALU.mult, ALU.add)\
                    .then_inc(var_done, 1)

            def finish(i, c):
                dve.wait_ge(std_done, i * C + c + 1)
                dve.reciprocal(rstd[:, c, :], std[:, c, :]).then_inc(rstd_done, 1)
                xn_free(dve, i, c)
                dve.wait_ge(rstd_done, i * C + c + 1)
                normalise(dve, c, range(G - 1))

            dve.memset(eps[:, :], EPS).then_inc(consts, 1)
            dve.memset(psL[:, :], 0.0).then_inc(consts, 1)
            with dve.Fori(0, TURNS) as i:
                for c in range(C):
                    statistics(i, c)
                    if c:
                        finish(i, c - 1)
                finish(i, C - 1)
            dve.wait_ge(b1_t, 1)
            dve.tensor_copy(m.b1T[:, :], psB[:, 0:E * HC])

        @block.scalar
        def _(act):
            act.dma_start(wgs[:, :, :], wg.rearrange("(k p) e -> p k e", p=P)).then_inc(wg_in, 16)
            act.dma_start(raw_b1[:, :], b1.rearrange("e (c p) -> (e c) p", p=P)).then_inc(w_in, 16)
            act.dma_start(m.raw_qkv[:, :, :], w_qkv.rearrange("(k p) n -> p k n", p=P)).then_inc(w_in, 16)
            act.dma_start(m.raw_out[:, :, :], w_out.rearrange("(k p) n -> p k n", p=P)).then_inc(w_in, 16)
            for e in range(E):
                act.dma_start(m.b2b[:, e, :], b2[e:e + 1, :].broadcast_to([P, D])).then_inc(w_in, 16)
            act.sem_inc(xT_done, 4)
            act.sem_inc(lT_copied, 1)
            act.sem_inc(l_copied, 1)
            act.wait_ge(consts, 3)

            def roots(i, c):
                act.wait_ge(var_done, i * C + c + 1)
                act.activation(std[:, c, :], var[:, c, :], ACT.Sqrt, bias=eps[:, 0:1]).then_inc(std_done, 1)

            with act.Fori(0, TURNS) as i:
                roots(i, 0)
                for c in range(C):
                    if c + 1 < C:
                        roots(i, c + 1)
                    if c == 0:
                        act.wait_ge(lT_done, i + 1)
                    for k in range(KD):
                        act.wait_ge(t_done, (i + 1) * TD + c * KD + k + 1)
                        act.activation(xT[:, c, k, :], psT[c % 2 * 2 + k][:, :], ACT.Copy).then_inc(xT_done, 1)
                act.wait_ge(lT_done, i + 2)
                act.activation(lT[:, :], psL[:, :], ACT.Copy).then_inc(lT_copied, 1)
                act.wait_ge(l_done, i + 1)
                act.activation(m.logits[:, bass.ds(i * C * G, C * G), :].rearrange("p (c j) e -> p j c e", c=C),
                               psX[:, :].rearrange("p (j c r) -> p j c r", j=G, c=C)[:, :, :, 0:E],
                               ACT.Copy).then_inc(l_copied, 1)

        @block.tensor
        def _(pe):
            pe.sem_inc(t_done, TD)
            pe.sem_inc(lT_done, 1)
            pe.wait_ge(consts, 3)
            pe.wait_ge(wg_in, 16)
            with pe.Fori(0, TURNS) as i:
                for c in range(C):
                    pe.wait_ge(norm_done[c], G * (i + 1))
                    pe.wait_ge(xT_done, i * TD + KD * (c + 1))
                    for k in range(KD):
                        for j in range(G):
                            last = pe.transpose(psT[c % 2 * 2 + k][:, j * P:(j + 1) * P],
                                                xnb[c][:, j, k * P:(k + 1) * P], m.eye[:, :])
                        last.then_inc(t_done, 1)
                pe.wait_ge(xT_done, 4 + (i + 1) * TD)
                pe.wait_ge(lT_copied, i + 1)
                for k in range(KD):
                    for c in range(C):
                        last = pe.matmul(psL[32 * c:32 * c + E, :], wgs[:, k, :], xT[:, c, k, :],
                                         start=(k == 0), stop=(k == KD - 1))
                last.then_inc(lT_done, 1)
                pe.wait_ge(lT_copied, i + 2)
                pe.wait_ge(l_copied, i + 1)
                for j in range(G):
                    last = pe.transpose(psX[:, j * P:(j + 1) * P], lT[:, j * P:(j + 1) * P], m.eye[:, :])
                last.then_inc(l_done, 1)
            pe.wait_ge(w_in, 16 * (3 + E))
            pe.transpose(psB[:, 0:E * HC], raw_b1[:, :], m.eye[0:E * HC, 0:E * HC]).then_inc(b1_t, 1)


def route_phase(nc, m, w1, w2):
    C = K * NT
    ctx = ExitStack()
    with ctx:
        sb = lambda n, s, d: ctx.enter_context(nc.sbuf_tensor(n, s, d))
        sem = lambda n: ctx.enter_context(nc.semaphore(n))
        ps = lambda n: ctx.enter_context(nc.psum_tensor(n, [P, 512], fp32))
        t8 = lambda n: sb(n, [P, NT, E], fp32)
        tc = lambda n, d=fp32: sb(n, [P, C], d)
        shifted, ex, score, tmp, tmp2, oh = t8("r_sh"), t8("r_ex"), t8("r_sc"), t8("r_t"), t8("r_t2"), t8("r_oh")
        red = sb("r_red", [P, NT], fp32)
        topv = sb("r_topv", [P, K, NT], fp32)
        den = sb("r_den", [P, NT], fp32)
        OH = sb("r_OH", [P, E, C], fp32)
        OHb = sb("r_OHb", [P, E, C], bf16)
        cum = sb("r_cum", [P, E, C], fp32)
        pos8 = sb("r_pos8", [P, E, C], fp32)
        ones_c = tc("r_ones")
        eid, pos, valid, kept, slotf, dslot = tc("r_eid"), tc("r_pos"), tc("r_valid"), tc("r_kept"), tc("r_slotf"), tc("r_ds")
        dint, aint, bint = tc("r_di", i32), tc("r_ai", i32), tc("r_bi", i32)
        af, bf = tc("r_af", bf16), tc("r_bf", bf16)
        tri = sb("r_tri", [P, P], bf16)
        ones = sb("r_onesb", [P, P], bf16)
        zeros = sb("r_zeros", [P, P], bf16)
        iota_e = sb("r_iota_e", [P, E], fp32)
        iota_e8 = sb("r_iota_e8", [P, E], fp32)
        iota_p = sb("r_iota_p", [P, 1], fp32)
        iota_t = sb("r_iota_t", [P, K, NT], bf16)
        iota_b = sb("r_iota_b", [P, P], bf16)
        R = 16
        ohB = sb("r_ohB", [P, 2, R, P], bf16)
        ohA = sb("r_ohA", [P, 2, R, E * ST], bf16)
        ohV = sb("r_ohV", [P, 2, R, 2, E * ST], bf16)
        tabp = sb("r_tabp", [P, E * ST], fp32)
        pre_ps, tot_ps, tab_ps = ps("r_pre"), ps("r_tot"), ps("r_tab")
        consts = sem("r_consts")
        chain = sem("r_chain")
        sh_done = sem("r_sh_done")
        ex_done = sem("r_ex_done")
        oh_done = sem("r_oh_done")
        sums_done = sem("r_sums")
        hot_a, hot_b, hot_tile, hot_place = (sem(f"r_hot_{n}") for n in ("a", "b", "tile", "place"))
        w_in, high, split = sem("r_w_in"), sem("r_high"), sem("r_split")
        hot_used = sem("r_hot_used")
        tab_done = sem("r_tab_done")
        block = ctx.enter_context(nc.Block())
        wide = lambda t, g, n: t[:, g * R:(g + 1) * R].unsqueeze(2).broadcast_to([P, R, n])
        to_split = [(m.raw_qkv, m.wqkv_h, m.wqkv_l), (m.raw_out, m.wout_h, m.wout_l), (m.raw1, m.w1h, m.w1l)]

        @block.sync
        def _(sp):
            sp.dma_start(m.raw1[:, :, :], w1[0].rearrange("(k p) h -> p k h", p=P)).then_inc(w_in, 16)
            sp.dma_start(m.raw2[:, :, :], w2[0].rearrange("(c p) d -> p c d", p=P)).then_inc(w_in, 16)
            sp.wait_ge(w_in, 32)

        @block.gpsimd
        def _(pool):
            pool.memset(zeros[:, :], 0.0).then_inc(consts, 1)
            pool.memset(ones[:, :], 1.0).then_inc(consts, 1)
            pool.memset(ones_c[:, :], 1.0).then_inc(consts, 1)
            pool.wait_ge(consts, 3)
            pool.affine_select(out=tri[:, :], in_=ones[:, :], compare_op=ALU.is_gt, fill=0.0, base=0,
                               pattern=[[1, P]], channel_multiplier=-1).then_inc(consts, 1)
            it = dict(allow_small_or_imprecise_dtypes=True)
            pool.iota(iota_e[:, :], pattern=[[1, E]], base=0, channel_multiplier=0, **it).then_inc(consts, 1)
            pool.iota(iota_e8[:, :], pattern=[[1, E]], base=-E, channel_multiplier=0, **it).then_inc(consts, 1)
            pool.iota(iota_p[:, :], pattern=[[1, 1]], base=0, channel_multiplier=1, **it).then_inc(consts, 1)
            pool.iota(iota_t[:, :, :], pattern=[[0, K], [1, NT]], base=0, channel_multiplier=0, **it).then_inc(consts, 1)
            pool.iota(iota_b[:, :], pattern=[[1, P]], base=0, channel_multiplier=0, **it).then_inc(consts, 1)
            for i, (raw, high_part, low_part) in enumerate(to_split):
                pool.wait_ge(high, i + 1)
                pool.tensor_tensor(low_part[:, :, :], raw[:, :, :], high_part[:, :, :].bitcast(fp32), ALU.subtract)\
                    .then_inc(split, 1)
            for g in range(C // R):
                pool.wait_ge(hot_a, g + 1)
                if g >= 2:
                    pool.wait_ge(hot_used, g - 1)
                pool.tensor_tensor(ohV[:, g % 2, :, 0, :], ohA[:, g % 2, :, :],
                                   wide(iota_t[:, :, :].rearrange("p k t -> p (k t)"), g, E * ST), ALU.mult)\
                    .then_inc(hot_tile, 1)

        @block.scalar
        def _(act):
            act.wait_ge(sh_done, 1)
            act.activation(ex[:, :, :], shifted[:, :, :], ACT.Exp).then_inc(ex_done, 1)
            for i, (raw, high_part, _) in enumerate(to_split):
                if raw is m.raw1:
                    act.wait_ge(w_in, 32)
                act.activation(high_part[:, :, :], raw[:, :, :], ACT.Copy).then_inc(high, 1)
            for g in range(C // R):
                act.wait_ge(hot_a, g + 1)
                if g >= 2:
                    act.wait_ge(hot_used, g - 1)
                act.activation(ohV[:, g % 2, :, 1, :], ohA[:, g % 2, :, :], ACT.Copy, scale=iota_p[:, 0:1])\
                    .then_inc(hot_place, 1)

        @block.tensor
        def _(pe):
            pe.wait_ge(consts, 9)
            pe.wait_ge(oh_done, 1)
            flat = OHb[:, :, :].rearrange("p e c -> p (e c)")
            pe.matmul(pre_ps[:, :], tri[:, :], flat, start=True, stop=True)
            pe.matmul(tot_ps[:, :], ones[:, :], flat, start=True, stop=True).then_inc(sums_done, 1)
            pe.matmul(tab_ps[:, 0:2 * E * ST], zeros[:, :], zeros[:, :], start=True, stop=False)
            for g in range(C // R):
                for part in (hot_b, hot_tile, hot_place):
                    pe.wait_ge(part, g + 1)
                for r in range(R):
                    last = pe.matmul(tab_ps[:, 0:2 * E * ST], ohB[:, g % 2, r, :],
                                     ohV[:, g % 2, r, :, :].rearrange("p a c -> p (a c)"), start=False, stop=False)
                last.then_inc(hot_used, 1)
            pe.matmul(tab_ps[:, 0:2 * E * ST], zeros[:, :], zeros[:, :], start=False, stop=True).then_inc(tab_done, 1)

        @block.vector
        def _(dve):
            count = [0]

            def link(ins):
                count[0] += 1
                ins.then_inc(chain, 1)
                dve.wait_ge(chain, count[0])

            tokb = lambda t: t.unsqueeze(2).broadcast_to([P, NT, E])
            expb = lambda t: t.unsqueeze(1).broadcast_to([P, NT, E])
            link(dve.tensor_reduce(red[:, :], m.logits[:, :, :], AX.X, ALU.max))
            dve.tensor_tensor(shifted[:, :, :], m.logits[:, :, :], tokb(red[:, :]), ALU.subtract).then_inc(sh_done, 1)
            dve.wait_ge(ex_done, 1)
            link(dve.tensor_reduce(red[:, :], ex[:, :, :], AX.X, ALU.add))
            link(dve.reciprocal(red[:, :], red[:, :]))
            link(dve.tensor_tensor(score[:, :, :], ex[:, :, :], tokb(red[:, :]), ALU.mult))
            dve.wait_ge(consts, 9)
            for k in range(K):
                link(dve.tensor_reduce(topv[:, k, :], score[:, :, :], AX.X, ALU.max))
                link(dve.tensor_tensor(tmp[:, :, :], score[:, :, :], tokb(topv[:, k, :]), ALU.is_equal))
                link(dve.tensor_tensor(tmp2[:, :, :], tmp[:, :, :], expb(iota_e8[:, :]), ALU.mult))
                link(dve.tensor_reduce(red[:, :], tmp2[:, :, :], AX.X, ALU.min))
                link(dve.tensor_tensor(oh[:, :, :], expb(iota_e8[:, :]), tokb(red[:, :]), ALU.is_equal))
                link(dve.tensor_copy(OH[:, :, k * NT:(k + 1) * NT].rearrange("p e t -> p t e"), oh[:, :, :]))
                if k == 0:
                    link(dve.scalar_tensor_tensor(score[:, :, :], oh[:, :, :], -4.0, score[:, :, :],
                                                  ALU.mult, ALU.add))
            dve.tensor_copy(OHb[:, :, :], OH[:, :, :]).then_inc(oh_done, 1)
            link(dve.tensor_tensor(den[:, :], topv[:, 0, :], topv[:, 1, :], ALU.add))
            link(dve.reciprocal(den[:, :], den[:, :]))
            link(dve.tensor_tensor(topv[:, :, :], topv[:, :, :], den[:, :].unsqueeze(1).broadcast_to([P, K, NT]),
                                   ALU.mult))
            dve.wait_ge(sums_done, 1)
            tot = tot_ps[:, :].rearrange("p (e c) -> p e c", e=E)
            for e in range(E):
                link(dve.tensor_tensor_scan(cum[:, e, :], ones_c[:, :], tot[:, e, :], 0.0, ALU.mult, ALU.add))
            link(dve.tensor_tensor(pos8[:, :, :], cum[:, :, :], tot, ALU.subtract))
            link(dve.tensor_tensor(cum[:, :, :], pos8[:, :, :],
                                   pre_ps[:, :].rearrange("p (e c) -> p e c", e=E), ALU.add))
            link(dve.tensor_tensor(pos8[:, :, :], cum[:, :, :], OH[:, :, :], ALU.mult))
            link(dve.tensor_reduce(pos[:, :], pos8[:, :, :].rearrange("p e c -> p c e"), AX.X, ALU.add))
            link(dve.tensor_tensor(cum[:, :, :], OH[:, :, :],
                                   iota_e[:, :].unsqueeze(2).broadcast_to([P, E, C]), ALU.mult))
            link(dve.tensor_reduce(eid[:, :], cum[:, :, :].rearrange("p e c -> p c e"), AX.X, ALU.add))
            link(dve.tensor_scalar(valid[:, :], pos[:, :], float(CAP), None, ALU.is_lt))
            link(dve.tensor_tensor(m.gates[:, :], topv[:, :, :].rearrange("p k t -> p (k t)"), valid[:, :], ALU.mult))
            link(dve.tensor_tensor(kept[:, :], pos[:, :], valid[:, :], ALU.mult))
            link(dve.scalar_tensor_tensor(slotf[:, :], eid[:, :], float(CAP), kept[:, :], ALU.mult, ALU.add))
            link(dve.tensor_copy(m.slots[:, :], slotf[:, :]))
            link(dve.tensor_scalar(valid[:, :], valid[:, :], -2.0 * E * CAP, 2.0 * E * CAP, ALU.mult, ALU.add))
            link(dve.tensor_tensor(dslot[:, :], slotf[:, :], valid[:, :], ALU.add))
            link(dve.tensor_copy(dint[:, :], dslot[:, :]))
            link(dve.tensor_single_scalar(aint[:, :], dint[:, :], 7, ALU.arith_shift_right))
            link(dve.tensor_single_scalar(bint[:, :], dint[:, :], P - 1, ALU.bitwise_and))
            link(dve.tensor_copy(af[:, :], aint[:, :]))
            link(dve.tensor_copy(bf[:, :], bint[:, :]))

            for g in range(C // R):
                if g >= 2:
                    dve.wait_ge(hot_used, g - 1)
                dve.tensor_tensor(ohA[:, g % 2, :, :], iota_b[:, 0:E * ST].unsqueeze(1).broadcast_to([P, R, E * ST]),
                                  wide(af, g, E * ST), ALU.is_equal).then_inc(hot_a, 1)
                dve.tensor_tensor(ohB[:, g % 2, :, :], iota_b[:, :].unsqueeze(1).broadcast_to([P, R, P]),
                                  wide(bf, g, P), ALU.is_equal).then_inc(hot_b, 1)
            dve.wait_ge(tab_done, 1)
            link(dve.tensor_copy(tabp[:, :], tab_ps[:, E * ST:2 * E * ST]))
            link(dve.scalar_tensor_tensor(m.token_of[:, :], tab_ps[:, 0:E * ST], float(P), tabp[:, :],
                                          ALU.mult, ALU.add))


def moe_phase(nc, m, xn_dram, w1, w2, y_dram):
    YR, FR = 4, 4
    ctx = ExitStack()
    with ctx:
        sb = lambda n, s, d: ctx.enter_context(nc.sbuf_tensor(n, s, d))
        sem = lambda n: ctx.enter_context(nc.semaphore(n))
        ps = lambda n: ctx.enter_context(nc.psum_tensor(n, [P, 512], fp32))
        raw1, raw2, w1h, w1l = m.raw1, m.raw2, m.w1h, m.w1l
        w2h, w2l = sb("m_w2h", [P, HC, D], fp32r), sb("m_w2l", [P, HC, D], fp32r)
        idx = sb("m_idx", [P, ST], u32)
        xg = [sb(f"m_xg{j}", [P, D], fp32) for j in range(ST)]
        xh, xl = sb("m_xh", [P, KD, CAP], fp32r), sb("m_xl", [P, KD, CAP], fp32r)
        hf = sb("m_hf", [P, FR, HALF], fp32)
        hh, hl = sb("m_hh", [P, 2, HC, HALF], fp32r), sb("m_hl", [P, 2, HC, HALF], fp32r)
        yb = sb("m_y", [P, YR, D], fp32)
        psF = [ps(f"m_psF{i}") for i in range(4)]
        psY = [ps(f"m_psY{i}") for i in range(2)]
        psT = [ps(f"m_psT{i}") for i in range(2)]
        raw1_in, raw2_in = sem("m_raw1_in"), sem("m_raw2_in")
        w1h_done, w1l_done, w2h_done, w2l_done = (sem(f"m_{n}") for n in ("w1h_d", "w1l_d", "w2h_d", "w2l_d"))
        idx_done = sem("m_idx_done")
        xg_in = [sem(f"m_xg_in{j}") for j in range(ST)]
        t_done = sem("m_t_done")
        xh_done, xl_done = sem("m_xh_done"), sem("m_xl_done")
        f_done = sem("m_f_done")
        hh_done, hl_done = sem("m_hh_done"), sem("m_hl_done")
        y_done = sem("m_y_done")
        yb_done = sem("m_yb_done")
        y_out = [sem(f"m_y_out{i}") for i in range(YR)]
        U = 2 * HC
        TG = 2 * KD
        EARLY = {3: 0, 5: 1}
        LATE = {3: 2, 5: 3}
        w1v = w1.rearrange("e (k p) h -> p (e k) h", p=P)
        w2v = w2.rearrange("e (c p) d -> p (e c) d", p=P)
        yv = y_dram.rearrange("(s p) d -> p s d", p=P)
        block = ctx.enter_context(nc.Block())

        def experts(eng, body):
            with eng.Fori(0, E - 1) as e:
                body(e, False)
            body(E - 1, True)

        @block.sync
        def _(sp):
            sp.sem_inc(raw1_in, 16)
            sp.sem_inc(raw2_in, 16)

            def body(e, last):
                if not last:
                    alone(sp, w1h_done, e + 1)
                    alone(sp, w1l_done, e + 1)
                    sp.dma_start(raw1[:, :, :], w1v[:, bass.ds((e + 1) * KD, KD), :]).then_inc(raw1_in, 16)
                    alone(sp, w2h_done, e + 1)
                    alone(sp, w2l_done, e + 1)
                    sp.dma_start(raw2[:, :, :], w2v[:, bass.ds((e + 1) * HC, HC), :]).then_inc(raw2_in, 16)
                for s in range(ST):
                    alone(sp, yb_done, e * ST + s + 3)
                    sp.dma_start(yv[:, bass.ds(e * ST + s, 1), :], yb[:, s % YR:s % YR + 1, :]).then_inc(y_out[s % YR], 16)
            experts(sp, body)
            for r in range(YR):
                sp.wait_ge(y_out[r], 16 * E * ST // YR)

        @block.gpsimd
        def _(pool):
            def gathers(e, first):
                if not first:
                    alone(pool, t_done, e * TG)
                pool.tensor_copy(idx[:, :], m.token_of[:, bass.ds(e * ST, ST)]).then_inc(idx_done, 1)
                alone(pool, idx_done, e + 1)
                for j in range(ST):
                    pool.indirect_dma_start(xg[j][:, :], None, xn_dram,
                                            bass.IndirectOffsetOnAxis(ap=idx[:, j:j + 1], axis=0))\
                        .then_inc(xg_in[j], 16)
            def split_w2(e, first):
                if not first:
                    alone(pool, y_done, e * ST)
                alone(pool, raw2_in, (e + 1) * 16)
                pool.tensor_copy(w2h[:, :, :], raw2[:, :, :]).then_inc(w2h_done, 1)
                alone(pool, w2h_done, e + 1)
                pool.tensor_tensor(w2l[:, :, :], raw2[:, :, :], w2h[:, :, :].bitcast(fp32), ALU.subtract)\
                    .then_inc(w2l_done, 1)

            gathers(0, True)
            split_w2(0, True)
            with pool.Fori(1, E) as e:
                gathers(e, False)
                split_w2(e, False)

        @block.scalar
        def _(act):
            def w1_high(e):
                act.wait_ge(raw1_in, (e + 1) * 16)
                act.activation(w1h[:, :, :], raw1[:, :, :], ACT.Copy).then_inc(w1h_done, 1)

            def x_high(e, groups):
                for g in groups:
                    act.wait_ge(t_done, e * TG + g + 1)
                    act.activation(xh[:, g % KD, (g // KD) * HALF:(g // KD + 1) * HALF], psT[g % 2][:, :], ACT.Copy)\
                        .then_inc(xh_done, 1)

            act.sem_inc(w1h_done, 1)
            x_high(0, range(KD))

            def body(e, last):
                for u in range(U):
                    act.wait_ge(f_done, e * U + u + 1)
                    alone(act, hl_done, e * U + u + 1)
                    bias = m.b1T[:, bass.ds(e * HC + u % HC, 1)]
                    act.activation(hf[:, u % FR, :], psF[u % 4][:, :], ACT.Relu, bias=bias)
                    if u == 0:
                        alone(act, y_done, e * ST)
                    act.activation(hh[:, u // HC, u % HC, :], psF[u % 4][:, :], ACT.Relu, bias=bias)\
                        .then_inc(hh_done, 1)
                    if u in LATE:
                        x_high(e, (LATE[u],))
                if not last:
                    w1_high(e + 1)
                    x_high(e + 1, range(KD))
            experts(act, body)

        @block.vector
        def _(dve):
            def w1_low(e):
                dve.wait_ge(w1h_done, e + 1)
                dve.tensor_tensor(w1l[:, :, :], raw1[:, :, :], w1h[:, :, :].bitcast(fp32), ALU.subtract)\
                    .then_inc(w1l_done, 1)

            def x_low(e, groups):
                for g in groups:
                    k, half = g % KD, g // KD
                    dve.wait_ge(xh_done, e * TG + g + 1)
                    dve.tensor_tensor(xl[:, k, half * HALF:(half + 1) * HALF], psT[g % 2][:, :],
                                      xh[:, k, half * HALF:(half + 1) * HALF].bitcast(fp32), ALU.subtract)\
                        .then_inc(xl_done, 1)

            def y_row(e, s):
                dve.wait_ge(y_done, e * ST + s + 1)
                if s >= YR:
                    dve.wait_ge(y_out[s % YR], 16 * (2 * e + 1))
                else:
                    dve.wait_ge(y_out[s % YR], 32 * e)
                dve.tensor_tensor(yb[:, s % YR:s % YR + 1, :], psY[s % 2][:, 0:D].unsqueeze(1),
                                  m.b2b[:, bass.ds(e, 1), :], ALU.add).then_inc(yb_done, 1)

            dve.sem_inc(hl_done, FR)
            dve.sem_inc(yb_done, 2)
            dve.sem_inc(w1l_done, 1)
            x_low(0, range(KD))

            def body(e, last):
                for u in range(U):
                    dve.wait_ge(hh_done, e * U + u + 1)
                    dve.tensor_tensor(hl[:, u // HC, u % HC, :], hf[:, u % FR, :],
                                      hh[:, u // HC, u % HC, :].bitcast(fp32), ALU.subtract).then_inc(hl_done, 1)
                    if u in LATE:
                        x_low(e, (LATE[u],))
                for s in range(ST):
                    y_row(e, s)
                    if s == 1 and not last:
                        w1_low(e + 1)
                    if s in EARLY and not last:
                        x_low(e + 1, (EARLY[s],))
            experts(dve, body)

        @block.tensor
        def _(pe):
            def transposes(e, groups):
                for g in groups:
                    k, half = g % KD, g // KD
                    pe.wait_ge(xl_done, e * TG + g + 1)
                    for j in range(ST // 2):
                        if k == 0:
                            pe.wait_ge(xg_in[half * ST // 2 + j], (e + 1) * 16)
                        last = pe.transpose(psT[g % 2][:, j * P:(j + 1) * P],
                                            xg[half * ST // 2 + j][:, k * P:(k + 1) * P], m.eye[:, :])
                    last.then_inc(t_done, 1)

            pe.sem_inc(xl_done, 2)
            transposes(0, range(KD))

            def body(e, last):
                pe.wait_ge(w1h_done, e + 1)
                pe.wait_ge(w1l_done, e + 1)
                for u in range(U):
                    half, c = u // HC, u % HC
                    if c == 0:
                        pe.wait_ge(xl_done, e * TG + 2 + KD * (half + 1))
                    pe.wait_ge(hl_done, e * U + u + 1)
                    cols = slice(half * HALF, (half + 1) * HALF)
                    split_products(pe, psF[u % 4][:, :],
                                   [(w1h[:, k, c * P:(c + 1) * P], w1l[:, k, c * P:(c + 1) * P],
                                     xh[:, k, cols], xl[:, k, cols]) for k in range(KD)]).then_inc(f_done, 1)
                    if u in LATE:
                        transposes(e, (LATE[u],))
                pe.wait_ge(w2h_done, e + 1)
                pe.wait_ge(w2l_done, e + 1)
                for s in range(ST):
                    half, j = s // (ST // 2), s % (ST // 2)
                    if j == 0:
                        pe.wait_ge(hl_done, e * U + FR + HC * (half + 1))
                    pe.wait_ge(yb_done, e * ST + s + 1)
                    split_products(pe, psY[s % 2][:, 0:D],
                                   [(hh[:, half, c, j * P:(j + 1) * P], hl[:, half, c, j * P:(j + 1) * P],
                                     w2h[:, c, :], w2l[:, c, :]) for c in range(HC)]).then_inc(y_done, 1)
                    if s in EARLY and not last:
                        transposes(e + 1, (EARLY[s],))
            experts(pe, body)


def attention_phase(nc, m, x, xn_dram, y_dram, out):
    UT = L // 2 // P
    UL = UT * P
    UB = UL // WIN
    BLK = 4
    STEPS = NH // 2 * UB // BLK
    UNITS = B * 2
    LAG_T, LAG_C, LAG_V, LAG_O = 3, 4, 5, 7
    LAG_I = 1
    LAG_Y = 3
    ITEMS = [("x", 0), ("x", 1), ("q", 0), ("k", 0), ("q", 1), ("k", 1)] + \
        [("o", t) for t in range(UT)] + [("v", t) for t in range(UT)]
    NI = len(ITEMS)
    O_FIRST = 2 + 2 * KD
    PRO = NI - UT
    PARTS = {"x": UT, "q": 3 * KD, "k": 3 * KD, "o": 3 * KD, "v": 3 * KD}
    COST = {"x": 0.5, "q": 1, "k": 1, "o": 0.5, "v": 0.5}
    SHARE = [4, 0, 4, 4, 4, 4, 4, 4] + [3] * 8
    parts_at, done_at = [[] for _ in range(STEPS)], [[] for _ in range(STEPS)]
    at, spent = 0, 0
    for i, (kind, _) in enumerate(ITEMS):
        for part in range(PARTS[kind]):
            while at < STEPS - 1 and spent >= sum(SHARE[:at + 1]) - 1e-6:
                at += 1
            parts_at[at].append((i, part))
            spent += COST[kind]
        done_at[at].append(i)
    PR, PTR, YG = 8, 8, 4
    GRP = 4
    ctx = ExitStack()
    with ctx:
        sb = lambda n, s, d: ctx.enter_context(nc.sbuf_tensor(n, s, d))
        sem = lambda n: ctx.enter_context(nc.semaphore(n))
        ps = lambda n: ctx.enter_context(nc.psum_tensor(n, [P, 512], fp32))
        two = lambda n: [sem(f"{n}{i}") for i in range(2)]
        xnr = sb("a_xn", [P, UT, D], fp32)
        xTh, xTl = sb("a_xTh", [P, KD, UL], fp32r), sb("a_xTl", [P, KD, UL], fp32r)
        qz = [sb(f"a_q{u}", [P, 2, UB, 2, WIN], fp32) for u in range(2)]
        kT = [sb(f"a_k{u}", [P, 2, WIN + UL], fp32) for u in range(2)]
        va = [sb(f"a_va{u}", [P, UT, D], fp32) for u in range(2)]
        vs = [sb(f"a_vs{u}", [P, UT, D], fp32) for u in range(2)]
        parity = sb("a_parity", [P, 2], fp32)
        pr = sb("a_p", [P, PR, BLK, P], fp32)
        nmax = sb("a_nmax", [P, PR, BLK], fp32)
        sums = sb("a_sums", [P, PR, BLK], fp32)
        rsum = sb("a_rsum", [P, PR, BLK], fp32)
        pT = sb("a_pT", [P, PTR, BLK, P], fp32)
        of = sb("a_o", [P, 2, BLK, WIN], fp32)
        oTh = [sb(f"a_oTh{u}", [P, KD, UL], fp32r) for u in range(2)]
        oTl = [sb(f"a_oTl{u}", [P, KD, UL], fp32r) for u in range(2)]
        res = [sb(f"a_res{u}", [P, UT, D], fp32) for u in range(2)]
        idx = [sb(f"a_idx{u}", [P, K, UT], u32) for u in range(2)]
        yg = [sb(f"a_yg{i}", [P, D], fp32) for i in range(YG)]
        psA = [ps("a_psA0"), ps("a_psA1")]
        psS = [ps("a_psS0"), ps("a_psS1")]
        psP = [ps("a_psP0"), ps("a_psP1")]
        psO = [ps("a_psO0"), ps("a_psO1")]
        zeroed = sem("a_zeroed")
        xn_in = sem("a_xn_in")
        item_done, item_free = two("a_item_done"), two("a_item_free")
        x_high = sem("a_x_high")
        shift_in = sem("a_shift_in")
        s_done = two("a_s_done")
        max_done, exp_done, rsum_done, norm_done = (sem(f"a_{n}") for n in ("max", "exp", "rsum", "norm"))
        t_done, pT_done = two("a_t_done"), two("a_pT_done")
        pv_done = sem("a_pv_done")
        o_even, o_free, o_high, o_low = (sem(f"a_o_{n}") for n in ("even", "free", "high", "low"))
        res_in, res_out = two("a_res_in"), two("a_res_out")
        idx_done = sem("a_idx_done")
        yg_in = [sem(f"a_yg_in{i}") for i in range(YG)]
        acc = sem("a_acc")
        xnv = xn_dram.rearrange("(t p) d -> p t d", p=P)
        xv = x.rearrange("b (t p) d -> p (b t) d", p=P)
        ov = out.rearrange("b (t p) d -> p (b t) d", p=P)
        block = ctx.enter_context(nc.Block())
        BS, HB = 2 * STEPS, NI

        def count(b, u, i, first, last):
            n = NI * u + PRO - UT + i
            if first and u == 0 and i < O_FIRST:
                n += UT
            if last and u == 1:
                n -= O_FIRST
            return b * HB + n // 2

        def there(t, i, first, last):
            u, (kind, j) = t // STEPS, ITEMS[i]
            if kind == "o" and first and u == 0 or kind != "o" and last and u == 1:
                return None
            return u, kind, j

        def ended(t, first, last):
            if t is None or t >= BS:
                return []
            return [(i,) + there(t, i, first, last) for i in done_at[t % STEPS] if there(t, i, first, last)]

        def batches(eng, body, tail):
            body(0, True, False)
            with eng.Fori(1, B - 1) as b:
                body(b, False, False)
            body(B - 1, False, True)
            tail(B - 1)

        def lagged(t, lag, first):
            return None if first and t < lag else t - lag

        def group_out(r):
            return psO[r][:, :].rearrange("p (n s t) -> p n s t", n=BLK, s=2)

        def o_cols(parts, g):
            i = g // GRP % (STEPS // GRP)
            cols = slice((i % 2) * BLK * WIN, (i % 2 + 1) * BLK * WIN)
            return parts[g // STEPS % 2][:, i // 2, cols].rearrange("p (n t) -> p n t", n=BLK)

        @block.sync
        def _(sp):
            sp.dma_start(xnr[:, :, :], xnv[:, 0:UT, :]).then_inc(xn_in, 16)
            sp.dma_start(res[0][:, :, :], xv[:, 0:UT, :]).then_inc(res_in[0], 16)
            sp.dma_start(res[1][:, :, :], xv[:, UT:2 * UT, :]).then_inc(res_in[1], 16)

            def shifts(u):
                sp.dma_start(vs[u][0:WIN, 0:1, :], va[1 - u][WIN:P, UT - 1:UT, :]).then_inc(shift_in, 16)
                sp.dma_start(vs[u][0:WIN, 1:UT, :], va[u][WIN:P, 0:UT - 1, :]).then_inc(shift_in, 16)
                sp.dma_start(vs[u][WIN:P, :, :], va[u][0:WIN, :, :]).then_inc(shift_in, 16)

            sp.wait_ge(item_done[1], 1)
            sp.dma_start(xnr[:, :, :], xnv[:, UT:2 * UT, :]).then_inc(xn_in, 16)
            sp.wait_ge(zeroed, 3)
            for i in range(2):
                sp.wait_ge(item_free[i], PRO // 2)
            shifts(0)

            def store(b, u, i, first, last):
                for j in (i - 1, i):
                    alone(sp, item_free[j % 2], count(b, u, j, first, last) + 1)
                sp.dma_start(ov[:, bass.ds(b * 2 * UT + (u - 1) * UT, UT), :], res[1 - u][:, :, :])\
                    .then_inc(res_out[1 - u], 16)

            def body(b, first, last):
                for u in range(2):
                    end = last and u == 1
                    if not (last and u >= 0):
                        alone(sp, item_done[1], count(b, u, 1, first, last) + 1)
                        sp.dma_start(xnr[:, :, :], xnv[:, bass.ds(b * 2 * UT + (u + 2) * UT, UT), :])\
                            .then_inc(xn_in, 16)
                    if not (first and u == 0):
                        store(b, u, O_FIRST + UT - 1, first, last)
                        if not end:
                            alone(sp, res_out[1 - u], 16 * (b + u))
                            sp.dma_start(res[1 - u][:, :, :], xv[:, bass.ds(b * 2 * UT + (u + 1) * UT, UT), :])\
                                .then_inc(res_in[1 - u], 16)
                    if not end:
                        for i in (NI - 2, NI - 1):
                            alone(sp, item_free[i % 2], count(b, u, i, first, last) + 1)
                        shifts(1 - u)

            def tail(b):
                for j in (NI - 2, NI - 1):
                    sp.wait_ge(item_free[j % 2], count(b, 1, j, False, True) + 1)
                sp.dma_start(ov[:, (UNITS - 1) * UT:UNITS * UT, :], res[1][:, :, :]).then_inc(res_out[1], 16)
                for u in range(2):
                    sp.wait_ge(res_out[u], 16 * B)
            batches(sp, body, tail)

        @block.gpsimd
        def _(pool):
            slots = m.slots[:, :].rearrange("p (k t) -> p k t", k=K)
            pool.memset(kT[1][:, :, UL:WIN + UL], 0.0)
            pool.memset(va[1][:, UT - 1, :], 0.0).then_inc(zeroed, 1)
            pool.tensor_copy(idx[0][:, :, :], slots[:, :, 0:UT]).then_inc(idx_done, 1)

            def body(b, first, last):
                for t in range(BS):
                    u, s, r = t // STEPS, t % STEPS, t % PR
                    alone(pool, rsum_done, b * BS + t + 1)
                    for j in range(BLK):
                        e = pr[:, r, j, :]
                        pool.tensor_scalar(e, e, rsum[:, r, j:j + 1], 0.0, ALU.mult, ALU.add).then_inc(norm_done, 1)
                    if s == 0:
                        alone(pool, idx_done, b * 2 + u + 1)
                    if s % 2 == 0:
                        i = s // 2
                        if not (first and u == 0 and i < YG):
                            alone(pool, acc, (b * 2 + u) * K * UT + i - YG + 1)
                        pool.indirect_dma_start(yg[i % YG][:, :], None, y_dram,
                                                bass.IndirectOffsetOnAxis(ap=idx[u][:, i % K, i // K:i // K + 1],
                                                                          axis=0)).then_inc(yg_in[i % YG], 16)
                    if s == STEPS // 2 and not (last and u == 1):
                        pool.tensor_copy(idx[1 - u][:, :, :],
                                         slots[:, :, bass.ds(b * 2 * UT + (u + 1) * UT, UT)]).then_inc(idx_done, 1)
            batches(pool, body, lambda b: None)

        @block.scalar
        def _(act):
            def read_item(kind, j, u, n, bank):
                if kind in "ko":
                    return
                act.wait_ge(item_done[bank], n + 1)
                if kind == "x":
                    act.activation(xTh[:, j, :], psA[bank][:, :], ACT.Copy).then_inc(x_high, 1)
                elif kind == "q":
                    for s in range(2):
                        ins = act.activation(qz[u][:, j, :, s, :], psA[bank][:, :].rearrange("p (n t) -> p n t", n=UB),
                                             ACT.Copy, scale=parity[:, s:s + 1])
                    ins.then_inc(item_free[bank], 1)
                else:
                    act.activation(va[u][:, j, :], psA[bank][:, 0:D], ACT.Copy).then_inc(item_free[bank], 1)

            act.wait_ge(zeroed, 3)
            for n in range(PRO):
                kind, j = ITEMS[n if n < O_FIRST else n + UT]
                read_item(kind, j, 0, n // 2, n % 2)

            def steps(b, ts, first, last):
                for t in ts:
                    g = lagged(t, LAG_O, first)
                    if g is not None and g < BS and g % GRP == GRP - 1:
                        r, n = g // GRP % 2, b * (BS // GRP) + g // GRP
                        act.wait_ge(pv_done, n + 1)
                        if not (first and g < 2 * GRP):
                            act.wait_ge(o_low, n - 1)
                        act.activation(of[:, r, :, :], group_out(r)[:, :, 0, :], ACT.Copy, scale=parity[:, 0:1])\
                            .then_inc(o_even, 1)
                    g = lagged(t, LAG_O + 1, first)
                    if g is not None and g % GRP == GRP - 1:
                        act.wait_ge(o_free, b * (BS // GRP) + g // GRP + 1)
                        act.activation(o_cols(oTh, g), of[:, g // GRP % 2, :, :], ACT.Copy).then_inc(o_high, 1)
                    for i, u, kind, j in ended(lagged(t, LAG_I, first), first, last):
                        if kind == "v" and j == 0:
                            act.wait_ge(shift_in, 48 * (b * 2 + u + 1))
                            if not (first and u == 0):
                                act.wait_ge(pv_done, (b * 2 + u) * (STEPS // GRP))
                        read_item(kind, j, (1 - u) % 2, count(b, u, i, first, last), i % 2)
                    if t < BS:
                        r = t % PR
                        for j in range(BLK):
                            act.wait_ge(max_done, (b * BS + t) * BLK + j + 1)
                            e = pr[:, r, j, :]
                            act.activation(e, e, ACT.Exp, scale=-1.0, bias=nmax[:, r, j:j + 1],
                                           accum_out=sums[:, r, j:j + 1]).then_inc(exp_done, 1)

            batches(act, lambda b, first, last: steps(b, range(BS), first, last),
                    lambda b: steps(b, range(BS, BS + LAG_O + 1), False, True))

        @block.vector
        def _(dve):
            for s in range(2):
                dve.tensor_reduce(parity[:, s:s + 1],
                                  m.eye[:, :].rearrange("p (g s d) -> p s g d", s=2, d=DH)[:, s], AX.XY, ALU.add)\
                    .then_inc(zeroed, 1)

            def read_item(kind, j, u, n, bank, xh_count):
                if kind == "x":
                    dve.wait_ge(x_high, xh_count)
                    dve.tensor_tensor(xTl[:, j, :], psA[bank][:, :], xTh[:, j, :].bitcast(fp32), ALU.subtract)\
                        .then_inc(item_free[bank], 1)
                elif kind == "k":
                    dve.tensor_copy(kT[u][:, j, 0:WIN], kT[1 - u][:, j, UL:UL + WIN])
                    dve.wait_ge(item_done[bank], n + 1)
                    dve.tensor_copy(kT[u][:, j, WIN:WIN + UL], psA[bank][:, :]).then_inc(item_free[bank], 1)

            dve.wait_ge(zeroed, 3)
            for n in range(PRO):
                kind, j = ITEMS[n if n < O_FIRST else n + UT]
                read_item(kind, j, 0, n // 2, n % 2, j + 1)

            def steps(b, ts, first, last):
                for t in ts:
                    if t < BS:
                        r = t % PR
                        if not (first and t < PR):
                            dve.wait_ge(t_done[t % 2], b * STEPS + (t - PR) // 2 + 1)
                        alone(dve, s_done[t % 2], b * STEPS + t // 2 + 1)
                        for j in range(BLK):
                            band = 1 if t < STEPS and t // GRP % 2 == 0 and j == 0 else 0
                            dve.tensor_tensor_reduce(
                                out=pr[:, r, j, :], in0=psS[t % 2][:, j * P:(j + 1) * P],
                                in1=m.mask[:, band, :], scale=-(DH ** -0.5), scalar=BIG,
                                op0=ALU.add, op1=ALU.min, accum_out=nmax[:, r, j:j + 1]).then_inc(max_done, 1)
                    g = lagged(t, 1, first)
                    if g is not None and g < BS:
                        dve.wait_ge(exp_done, (b * BS + g + 1) * BLK)
                        dve.reciprocal(rsum[:, g % PR, :], sums[:, g % PR, :]).then_inc(rsum_done, 1)
                    g = lagged(t, LAG_C, first)
                    if g is not None and g < BS:
                        dve.wait_ge(t_done[g % 2], b * STEPS + g // 2 + 1)
                        if not (first and g < PTR):
                            dve.wait_ge(pv_done, b * (BS // GRP) + (g - PTR) // GRP + 1)
                        dve.tensor_copy(pT[:, g % PTR, :, :].rearrange("p c q -> p (c q)"), psP[g % 2][:, :])\
                            .then_inc(pT_done[g % 2], 1)
                    for i, u, kind, j in ended(lagged(t, LAG_I, first), first, last):
                        n = count(b, u, i, first, last)
                        if kind == "o":
                            add_out((1 - u) % 2, j, n, i % 2, (b * 2 + u) * K * UT)
                        else:
                            read_item(kind, j, (1 - u) % 2, n, i % 2, (b * 2 + u + 1) * KD + j + 1)
                    g = lagged(t, LAG_Y, first)
                    if g is not None and g < BS and g % 2 == 0:
                        u, i = g // STEPS % 2, g % STEPS // 2
                        ub = b * 2 + g // STEPS
                        tile, k = i // K, i % K
                        if i == 0:
                            dve.wait_ge(res_in[u], 16 * (b + (g // STEPS + 2) // 2))
                        dve.wait_ge(yg_in[i % YG], 16 * (ub * (K * UT // YG) + i // YG + 1))
                        if k == 1:
                            dve.wait_ge(acc, ub * K * UT + i)
                        dve.scalar_tensor_tensor(res[u][:, tile, :], yg[i % YG][:, :],
                                                 m.gates[:, bass.ds(ub * UT + k * NT + tile, 1)],
                                                 res[u][:, tile, :], ALU.mult, ALU.add).then_inc(acc, 1)
                    g = lagged(t, LAG_O, first)
                    if g is not None and g < BS and g % GRP == GRP - 1:
                        r = g // GRP % 2
                        dve.wait_ge(o_even, b * (BS // GRP) + g // GRP + 1)
                        dve.scalar_tensor_tensor(of[:, r, :, :], group_out(r)[:, :, 1, :], parity[:, 1:2],
                                                 of[:, r, :, :], ALU.mult, ALU.add).then_inc(o_free, 1)
                    g = lagged(t, LAG_O + 1, first)
                    if g is not None and g % GRP == GRP - 1:
                        dve.wait_ge(o_high, b * (BS // GRP) + g // GRP + 1)
                        dve.tensor_tensor(o_cols(oTl, g), of[:, g // GRP % 2, :, :], o_cols(oTh, g).bitcast(fp32),
                                          ALU.subtract).then_inc(o_low, 1)

            def add_out(u, j, n, bank, sums_before):
                dve.wait_ge(acc, sums_before)
                dve.wait_ge(item_done[bank], n + 1)
                dve.tensor_tensor(res[u][:, j, :], res[u][:, j, :], psA[bank][:, 0:D], ALU.add)\
                    .then_inc(item_free[bank], 1)

            def tail(b):
                steps(b, range(BS, BS + LAG_O + 1), False, True)
                for j in range(UT):
                    add_out(1, j, count(b, 1, NI - UT + j, False, True), j % 2, UNITS * K * UT)
            batches(dve, lambda b, first, last: steps(b, range(BS), first, last), tail)

        @block.tensor
        def _(pe):
            def product(kind, j, u, n, bank, start, xn_count, o_count, parts):
                begins = parts[0] == 0
                if begins and not start:
                    pe.wait_ge(item_free[bank], n)
                if begins and kind == "x":
                    pe.wait_ge(xn_in, xn_count)
                if begins and kind == "q" and j == 0:
                    pe.wait_ge(item_free[1 - bank], n)
                if begins and kind == "o" and j == 0:
                    pe.wait_ge(o_low, o_count)
                out_ps = psA[bank]
                tile = slice(j * P, (j + 1) * P)
                for part in parts:
                    if kind == "x":
                        last = pe.transpose(out_ps[:, part * P:(part + 1) * P], xnr[:, part, j * P:(j + 1) * P],
                                            m.eye[:, :])
                        continue
                    k, low_l, low_r = part // 3, part % 3 == 2, part % 3 == 1
                    w = {"q": slice(j * P, (j + 1) * P), "k": slice(D + j * P, D + (j + 1) * P),
                         "v": slice(2 * D, 3 * D), "o": slice(0, D)}[kind]
                    wqkv = lambda low: (m.wqkv_l if low else m.wqkv_h)[:, k, w]
                    xT = lambda low: xTl if low else xTh
                    if kind in "qk":
                        args = out_ps[:, :], wqkv(low_l), xT(low_r)[:, k, :]
                    elif kind == "v":
                        args = out_ps[:, 0:D], xT(low_l)[:, k, tile], wqkv(low_r)
                    else:
                        args = out_ps[:, 0:D], (oTl if low_l else oTh)[u][:, k, tile], \
                            (m.wout_l if low_r else m.wout_h)[:, k, w]
                    last = pe.matmul(*args, start=part == 0, stop=part == 3 * KD - 1)
                if parts[-1] == PARTS[kind] - 1:
                    last.then_inc(item_done[bank], 1)

            pe.wait_ge(zeroed, 3)
            for n in range(PRO):
                kind, j = ITEMS[n if n < O_FIRST else n + UT]
                product(kind, j, 0, n // 2, n % 2, n < 2, 16, 0, range(PARTS[kind]))

            def scores(b, t, first):
                u, s = t // STEPS % 2, t % STEPS
                mt, half, rows = s // (2 * GRP), s // GRP % 2, slice(32 * (s % GRP), 32 * (s % GRP) + 32)
                if s == 0:
                    for i in (O_FIRST - 2, O_FIRST - 1):
                        pe.wait_ge(item_free[i % 2], i // 2 + 1 if first and t == 0 else
                                   count(b, t // STEPS - 1, i, first, False) + 1)
                if not (first and t < 2):
                    pe.wait_ge(max_done, (b * BS + t - 1) * BLK)
                for j in range(BLK):
                    blk = half * BLK + j
                    ins = pe.matmul(psS[t % 2][:, j * P:(j + 1) * P],
                                    qz[u][rows, mt, blk, :, :].rearrange("p s t -> p (s t)"),
                                    kT[u][rows, mt, blk * WIN:blk * WIN + 2 * WIN], start=True, stop=True)
                ins.then_inc(s_done[t % 2], 1)

            def steps(b, ts, first, last):
                for t in ts:
                    if t < BS - 1 or t == BS - 1 and not last:
                        scores(b, t + 1, first)
                    g = lagged(t, LAG_T, first)
                    if g is not None and g < BS:
                        pe.wait_ge(norm_done, (b * BS + g + 1) * BLK)
                        if not (first and g < 2):
                            pe.wait_ge(pT_done[g % 2], b * STEPS + g // 2)
                        for j in range(BLK):
                            ins = pe.transpose(psP[g % 2][:, j * P:(j + 1) * P], pr[:, g % PR, j, :], m.eye[:, :])
                        ins.then_inc(t_done[g % 2], 1)
                    g = lagged(t, LAG_V, first)
                    if g is not None and g < BS and g % GRP == GRP - 1:
                        s, r, n = g % STEPS, g // GRP % 2, b * (BS // GRP) + g // GRP
                        mt, half = s // (2 * GRP), s // GRP % 2
                        if s == GRP - 1:
                            pe.wait_ge(shift_in, 48 * (b * 2 + g // STEPS + 1))
                        for i in (0, 1):
                            pe.wait_ge(pT_done[i], b * STEPS + g // 2 + 1)
                        if not (first and g < 2 * GRP):
                            pe.wait_ge(o_free, n - 1)
                        for j in range(BLK):
                            blk = half * BLK + j
                            v = (va if blk % 2 else vs)[g // STEPS % 2]
                            for c in range(GRP):
                                heads = slice(mt * P + 32 * c, mt * P + 32 * (c + 1))
                                ins = pe.matmul(psO[r][32 * c:32 * (c + 1), j * P:(j + 1) * P],
                                                v[:, blk // 2, heads], pT[:, (g - GRP + 1 + c) % PTR, j, :],
                                                start=True, stop=True)
                        ins.then_inc(pv_done, 1)
                    if t < BS:
                        for i in range(NI):
                            parts = [part for item, part in parts_at[t % STEPS] if item == i]
                            if parts and there(t, i, first, last):
                                u, kind, j = there(t, i, first, last)
                                product(kind, j, 1 - u, count(b, u, i, first, last), i % 2, False,
                                        16 * (b * 2 + u + 2), (b * 2 + u) * (STEPS // GRP), parts)

            scores(0, 0, True)

            def tail(b):
                steps(b, range(BS, BS + LAG_V + 1), False, True)
                for j in range(UT):
                    product("o", j, 1, count(b, 1, NI - UT + j, False, True), j % 2, False, 0, B * (BS // GRP), range(3 * KD))
            batches(pe, lambda b, first, last: steps(b, range(BS), first, last), tail)


def build(nc, x, w_qkv, w_out, wg, w1, b1, w2, b2, out):
    ctx = ExitStack()
    with ctx:
        sb = lambda n, s, d: ctx.enter_context(nc.sbuf_tensor(n, s, d))
        xn_dram = nc.dram_tensor("xn_scratch", (N, D), fp32, kind="Internal").ap()
        y_dram = nc.dram_tensor("y_scratch", (E * CAP, D), fp32, kind="Internal").ap()
        m = Mem()
        Mem.passed = ctx.enter_context(nc.semaphore("waits_passed"))
        m.eye = sb("eye", [P, P], fp32)
        m.mask = sb("mask", [P, 2, 2 * WIN], fp32)
        m.logits = sb("logits", [P, NT, E], fp32)
        m.wqkv_h, m.wqkv_l = sb("wqkv_h", [P, KD, 3 * D], fp32r), sb("wqkv_l", [P, KD, 3 * D], fp32r)
        m.wout_h, m.wout_l = sb("wout_h", [P, KD, D], fp32r), sb("wout_l", [P, KD, D], fp32r)
        m.gates = sb("gates", [P, K * NT], fp32)
        m.slots = sb("slots", [P, K * NT], u32)
        m.token_of = sb("token_of", [P, E * ST], u32)
        with ExitStack() as inner:
            m.b1T = inner.enter_context(nc.sbuf_tensor("b1T", [P, E * HC], fp32))
            m.b2b = inner.enter_context(nc.sbuf_tensor("b2b", [P, E, D], fp32))
            m.raw1 = inner.enter_context(nc.sbuf_tensor("raw1", [P, KD, H], fp32))
            m.raw2 = inner.enter_context(nc.sbuf_tensor("raw2", [P, HC, D], fp32))
            m.w1h = inner.enter_context(nc.sbuf_tensor("w1h", [P, KD, H], fp32r))
            m.w1l = inner.enter_context(nc.sbuf_tensor("w1l", [P, KD, H], fp32r))
            with ExitStack() as early:
                m.raw_qkv = early.enter_context(nc.sbuf_tensor("raw_qkv", [P, KD, 3 * D], fp32))
                m.raw_out = early.enter_context(nc.sbuf_tensor("raw_out", [P, KD, D], fp32))
                norm_phase(nc, m, x, xn_dram, wg, w_qkv, w_out, b1, b2)
                route_phase(nc, m, w1, w2)
            moe_phase(nc, m, xn_dram, w1, w2, y_dram)
        attention_phase(nc, m, x, xn_dram, y_dram, out)


_INS = ['L0_attn_x', 'L0_attn_w_qkv', 'L0_attn_w_out', 'L0_ffn_wg', 'L0_ffn_w1', 'L0_ffn_b1', 'L0_ffn_w2',
        'L0_ffn_b2']


def kernel(**inputs):
    import numpy as _np
    import concourse.bacc as _bacc
    from concourse import mybir as _mybir
    from concourse.bass_utils import run_bass_kernel_spmd as _run

    nc = _bacc.Bacc("TRN2", target_bir_lowering=False, num_devices=1)
    arrays, args = {}, []
    for name in _INS:
        a = _np.ascontiguousarray(inputs[name])
        arrays[f"in_{name}"] = a
        args.append(nc.dram_tensor(f"in_{name}", a.shape, _mybir.dt.from_np(a.dtype), kind="ExternalInput").ap())
    o = nc.dram_tensor("out_0", (B, L, D), fp32, kind="ExternalOutput").ap()
    build(nc, *args, o)
    r = _run(nc, [arrays], core_ids=[0])
    return r.results[0]["out_0"]
```

```python
import concourse.bass as bass
from concourse import mybir
from contextlib import ExitStack

fp32 = mybir.dt.float32
fp32r = mybir.dt.float32r
bf16 = mybir.dt.bfloat16
u32 = mybir.dt.uint32
i32 = mybir.dt.int32
ALU = mybir.AluOpType
ACT = mybir.ActivationFunctionType
AX = mybir.AxisListType

P = 128
B, L, D = 4, 1024, 256
N = B * L
KD = D // P
NT = N // P
E, K, H = 8, 2, 1024
CAP = K * N // E
HC = H // P
ST = CAP // P
HALF = CAP // 2
NH, DH, WIN = 16, 16, 64
NB = L // WIN
NEG = -1e30
EPS = 1e-5
BIG = 3e38


class Mem:
    pass


def alone(eng, sem, value):
    eng.wait_ge(sem, value)
    eng.sem_inc(Mem.passed, 1)


def split_products(pe, out, pairs, n_start=True, n_stop=True):
    last, n = None, 3 * len(pairs)
    i = 0
    for lh, ll, rh, rl in pairs:
        for a, b in ((lh, rh), (lh, rl), (ll, rh)):
            last = pe.matmul(out, a, b, start=(n_start and i == 0), stop=(n_stop and i == n - 1))
            i += 1
    return last


def norm_phase(nc, m, x, xn_dram, wg, b1):
    G, C = 4, 4
    TURNS = NT // (G * C)
    ctx = ExitStack()
    with ctx:
        sb = lambda n, s, d: ctx.enter_context(nc.sbuf_tensor(n, s, d))
        sem = lambda n: ctx.enter_context(nc.semaphore(n))
        ps = lambda n: ctx.enter_context(nc.psum_tensor(n, [P, 512], fp32))
        each = lambda n: [sem(f"{n}{c}") for c in range(C)]
        xin = [sb(f"n_xin{c}", [P, TURNS * G, D], fp32) for c in range(C)]
        xnb = [sb(f"n_xn{c}", [P, TURNS * G, D], fp32) for c in range(C)]
        stats = sb("n_stats", [P, C, G, 6], fp32)
        total, gap, spread, gap2, mean, var, std, rstd = (
            sb(f"n_{n}", [P, C, G], fp32) for n in ("total", "gap", "spread", "gap2", "mean", "var", "std", "rstd"))
        eps = sb("n_eps", [P, 1], fp32)
        xT = sb("n_xT", [P, C, KD, G * P], fp32)
        lT = sb("n_lT", [P, G * P], fp32)
        wgs = sb("n_wg", [P, KD, E], fp32)
        raw_b1 = sb("n_rawb1", [E * HC, P], fp32)
        psT = [ps(f"n_psT{i}") for i in range(4)]
        psL, psX, psB = ps("n_psL"), ps("n_psX"), ps("n_psB")
        x_in = [sem(f"n_x_in{i}") for i in range(TURNS * C)]
        norm_done, xn_out = each("n_norm_done"), sem("n_xn_out")
        wg_in, w_in = sem("n_wg_in"), sem("n_w_in")
        consts, made, chain = sem("n_consts"), sem("n_made"), sem("n_chain")
        var_done, std_done, rstd_done = sem("n_var_done"), sem("n_std_done"), sem("n_rstd_done")
        t_done, xT_done = sem("n_t_done"), sem("n_xT_done")
        lT_done, lT_copied, l_done, l_copied = sem("n_lT_done"), sem("n_lT_copied"), sem("n_l_done"), sem("n_l_copied")
        b1_t = sem("n_b1_t")
        xv = x.rearrange("b (t p) d -> p (b t) d", p=P)
        xnv = xn_dram.rearrange("(t p) d -> p t d", p=P)
        block = ctx.enter_context(nc.Block())
        TD = KD * C

        def normalise(eng, i, c, tiles):
            for j in tiles:
                eng.tensor_scalar(xnb[c][:, i * G + j, :], xin[c][:, i * G + j, :], mean[:, c, j:j + 1], rstd[:, c, j:j + 1],
                                  ALU.subtract, ALU.mult).then_inc(norm_done[c], 1)

        @block.sync
        def _(sp):
            for i in range(TURNS):
                for c in range(C):
                    t = (i * C + c) * G
                    sp.dma_start(xin[c][:, i * G:(i + 1) * G, :], xv[:, t:t + G, :]).then_inc(x_in[i * C + c], 16)
            for i in range(TURNS):
                for c in range(C):
                    sp.wait_ge(norm_done[c], G * (i + 1))
                    t = (i * C + c) * G
                    sp.dma_start(xnv[:, t:t + G, :], xnb[c][:, i * G:(i + 1) * G, :]).then_inc(xn_out, 16)
            sp.wait_ge(xn_out, 16 * TURNS * C)

        @block.gpsimd
        def _(pool):
            pool.memset(m.eye[:, :], 0.0).then_inc(made, 1)
            pool.wait_ge(made, 1)
            pool.affine_select(out=m.eye[:, :], in_=m.eye[:, :], compare_op=ALU.not_equal, fill=1.0,
                               base=0, pattern=[[-1, P]], channel_multiplier=1).then_inc(consts, 1)
            for i in range(TURNS):
                for c in range(C):
                    alone(pool, rstd_done, i * C + c + 1)
                    normalise(pool, i, c, (G - 1,))
            pool.memset(m.mask[:, :, :], 0.0).then_inc(made, 1)
            n = 2
            for sign in (1, -1):
                pool.wait_ge(made, n)
                for first in range(2):
                    for s in range(2):
                        part = m.mask[s * WIN:(s + 1) * WIN, first, :]
                        pool.affine_select(out=part, in_=part, compare_op=ALU.is_ge, fill=NEG,
                                           base=-1 if sign == 1 else WIN, pattern=[[sign, 2 * WIN]],
                                           channel_multiplier=-sign).then_inc(made, 1)
                        n += 1
            pool.wait_ge(made, n)
            pool.memset(m.mask[:, 1, 0:WIN], NEG)

        @block.vector
        def _(dve):
            LINKS = 3 * C

            def link(ins, value):
                ins.then_inc(chain, 1)
                dve.wait_ge(chain, value)

            def statistics(i, c):
                dve.wait_ge(x_in[i * C + c], 16)
                for j in range(G):
                    ins = dve.bn_stats(stats[:, c, j, :], xin[c][:, i * G + j, :])
                n = i * LINKS + 3 * c
                link(ins, n + 1)
                even = lambda k: stats[:, c, :, k]
                dve.tensor_tensor(total[:, c, :], even(1), even(4), ALU.add)
                dve.tensor_tensor(gap[:, c, :], even(1), even(4), ALU.subtract)
                link(dve.tensor_tensor(spread[:, c, :], even(2), even(5), ALU.add), n + 2)
                dve.tensor_scalar(mean[:, c, :], total[:, c, :], 0.5, None, ALU.mult)
                link(dve.scalar_tensor_tensor(gap2[:, c, :], gap[:, c, :], 0.25, gap[:, c, :], ALU.mult, ALU.mult),
                     n + 3)
                dve.scalar_tensor_tensor(var[:, c, :], spread[:, c, :], 1.0 / D, gap2[:, c, :], ALU.mult, ALU.add)\
                    .then_inc(var_done, 1)

            def finish(i, c):
                dve.wait_ge(std_done, i * C + c + 1)
                dve.reciprocal(rstd[:, c, :], std[:, c, :]).then_inc(rstd_done, 1)
                dve.wait_ge(rstd_done, i * C + c + 1)
                normalise(dve, i, c, range(G - 1))

            dve.memset(eps[:, :], EPS).then_inc(consts, 1)
            dve.memset(psL[:, :], 0.0).then_inc(consts, 1)
            for n in range(TURNS * C + 1):
                if n < TURNS * C:
                    statistics(n // C, n % C)
                if n:
                    finish((n - 1) // C, (n - 1) % C)
            dve.wait_ge(consts, 3)
            for s in range(2):
                dve.tensor_reduce(m.parity[:, s:s + 1],
                                  m.eye[:, :].rearrange("p (g s d) -> p s g d", s=2, d=DH)[:, s], AX.XY, ALU.add)
            dve.wait_ge(b1_t, 1)
            dve.tensor_copy(m.b1T[:, :], psB[:, 0:E * HC])

        @block.scalar
        def _(act):
            act.dma_start(wgs[:, :, :], wg.rearrange("(k p) e -> p k e", p=P)).then_inc(wg_in, 16)
            act.dma_start(raw_b1[:, :], b1.rearrange("e (c p) -> (e c) p", p=P)).then_inc(w_in, 16)
            act.sem_inc(xT_done, 4)
            act.sem_inc(lT_copied, 1)
            act.sem_inc(l_copied, 1)
            act.wait_ge(consts, 3)

            def roots(i, c):
                act.wait_ge(var_done, i * C + c + 1)
                act.activation(std[:, c, :], var[:, c, :], ACT.Sqrt, bias=eps[:, 0:1]).then_inc(std_done, 1)

            def logits_out(i):
                act.wait_ge(lT_done, i + 2)
                act.activation(lT[:, :], psL[:, :], ACT.Copy).then_inc(lT_copied, 1)

            def logits_in(i):
                act.wait_ge(l_done, i + 1)
                act.activation(m.logits[:, i * C * G:(i + 1) * C * G, :].rearrange("p (c j) e -> p j c e", c=C),
                               psX[:, :].rearrange("p (j c r) -> p j c r", j=G, c=C)[:, :, :, 0:E],
                               ACT.Copy).then_inc(l_copied, 1)

            roots(0, 0)
            for n in range(TURNS * C):
                i, c = n // C, n % C
                if n + 1 < TURNS * C:
                    roots((n + 1) // C, (n + 1) % C)
                if c == 0 and i:
                    logits_out(i - 1)
                for k in range(KD):
                    act.wait_ge(t_done, (i + 1) * TD + c * KD + k + 1)
                    act.activation(xT[:, c, k, :], psT[c % 2 * 2 + k][:, :], ACT.Copy).then_inc(xT_done, 1)
                if c == 1 and i:
                    logits_in(i - 1)
            logits_out(TURNS - 1)
            logits_in(TURNS - 1)

        @block.tensor
        def _(pe):
            pe.sem_inc(t_done, TD)
            pe.sem_inc(lT_done, 1)
            pe.wait_ge(consts, 3)
            pe.wait_ge(wg_in, 16)
            for i in range(TURNS):
                for c in range(C):
                    pe.wait_ge(norm_done[c], G * (i + 1))
                    pe.wait_ge(xT_done, i * TD + KD * (c + 1))
                    for k in range(KD):
                        for j in range(G):
                            last = pe.transpose(psT[c % 2 * 2 + k][:, j * P:(j + 1) * P],
                                                xnb[c][:, i * G + j, k * P:(k + 1) * P], m.eye[:, :])
                        last.then_inc(t_done, 1)
                pe.wait_ge(xT_done, 4 + (i + 1) * TD)
                pe.wait_ge(lT_copied, i + 1)
                for k in range(KD):
                    for c in range(C):
                        last = pe.matmul(psL[32 * c:32 * c + E, :], wgs[:, k, :], xT[:, c, k, :],
                                         start=(k == 0), stop=(k == KD - 1))
                last.then_inc(lT_done, 1)
                pe.wait_ge(lT_copied, i + 2)
                pe.wait_ge(l_copied, i + 1)
                for j in range(G):
                    last = pe.transpose(psX[:, j * P:(j + 1) * P], lT[:, j * P:(j + 1) * P], m.eye[:, :])
                last.then_inc(l_done, 1)
            pe.wait_ge(w_in, 16)
            pe.transpose(psB[:, 0:E * HC], raw_b1[:, :], m.eye[0:E * HC, 0:E * HC]).then_inc(b1_t, 1)


def route_phase(nc, m, xn_dram, w_qkv, w_out, w1, w2, b2):
    C = K * NT
    ctx = ExitStack()
    with ctx:
        sb = lambda n, s, d: ctx.enter_context(nc.sbuf_tensor(n, s, d))
        sem = lambda n: ctx.enter_context(nc.semaphore(n))
        ps = lambda n: ctx.enter_context(nc.psum_tensor(n, [P, 512], fp32))
        t8 = lambda n: sb(n, [P, NT, E], fp32)
        tc = lambda n, d=fp32: sb(n, [P, C], d)
        shifted, ex, score, tmp, tmp2 = t8("r_sh"), t8("r_ex"), t8("r_sc"), t8("r_t"), t8("r_t2")
        red = sb("r_red", [P, NT], fp32)
        topv = sb("r_topv", [P, K, NT], fp32)
        den = sb("r_den", [P, NT], fp32)
        OH = sb("r_OH", [P, E, C], fp32)
        OHb = sb("r_OHb", [P, E, C], bf16)
        cum = sb("r_cum", [P, E, C], fp32)
        pos8 = sb("r_pos8", [P, E, C], fp32)
        ones_c = tc("r_ones")
        eid, pos, valid, kept, slotf, dslot = tc("r_eid"), tc("r_pos"), tc("r_valid"), tc("r_kept"), tc("r_slotf"), tc("r_ds")
        dint, aint, bint = tc("r_di", i32), tc("r_ai", i32), tc("r_bi", i32)
        af, bf = tc("r_af", bf16), tc("r_bf", bf16)
        tri = sb("r_tri", [P, P], bf16)
        ones = sb("r_onesb", [P, P], bf16)
        zeros = sb("r_zeros", [P, P], bf16)
        iota_e = sb("r_iota_e", [P, E], fp32)
        iota_e8 = sb("r_iota_e8", [P, E], fp32)
        iota_p = sb("r_iota_p", [P, 1], fp32)
        iota_t = sb("r_iota_t", [P, K, NT], bf16)
        iota_b = sb("r_iota_b", [P, P], bf16)
        R = 16
        ohB = sb("r_ohB", [P, 2, R, P], bf16)
        ohA = sb("r_ohA", [P, 2, R, E * ST], bf16)
        ohV = sb("r_ohV", [P, 2, R, 2, E * ST], bf16)
        tabp = sb("r_tabp", [P, E * ST], fp32)
        pre_ps, tot_ps, tab_ps = ps("r_pre"), ps("r_tot"), ps("r_tab")
        UT, UL = L // 2 // P, L // 2
        xTh, xTl = sb("r_xTh", [P, KD, UL], fp32r), sb("r_xTl", [P, KD, UL], fp32r)
        psA = [ps(f"r_psA{i}") for i in range(2)]
        xnr_in, x_high, x_low = sem("r_xnr_in"), sem("r_x_high"), sem("r_x_low")
        item_done, item_free = sem("r_item_done"), sem("r_item_free")
        consts = sem("r_consts")
        chain = sem("r_chain")
        sh_done = sem("r_sh_done")
        ex_done = sem("r_ex_done")
        oh_done = sem("r_oh_done")
        sums_done = sem("r_sums")
        hot_a, hot_b, hot_tile, hot_place = (sem(f"r_hot_{n}") for n in ("a", "b", "tile", "place"))
        w_in, late_in = [sem(f"r_w_in{i}") for i in range(3)], sem("r_late_in")
        high, split = sem("r_high"), sem("r_split")
        hot_used = sem("r_hot_used")
        tab_done = sem("r_tab_done")
        block = ctx.enter_context(nc.Block())
        assert C // R == UT
        wide = lambda t, g, n: t[:, g * R:(g + 1) * R].unsqueeze(2).broadcast_to([P, R, n])
        to_split = [(m.raw_qkv, m.wqkv_h, m.wqkv_l), (m.raw_out, m.wout_h, m.wout_l), (m.raw1, m.w1h, m.w1l)]

        @block.sync
        def _(sp):
            sp.dma_start(m.xnr[:, :, :], xn_dram.rearrange("(t p) d -> p t d", p=P)[:, 0:UT, :]).then_inc(xnr_in, 16)
            sp.dma_start(m.raw_qkv[:, :, :], w_qkv.rearrange("(k p) n -> p k n", p=P)).then_inc(w_in[0], 16)
            sp.dma_start(m.raw_out[:, :, :], w_out.rearrange("(k p) n -> p k n", p=P)).then_inc(w_in[1], 16)
            sp.dma_start(m.raw1[:, :, :], w1[0].rearrange("(k p) h -> p k h", p=P)).then_inc(w_in[2], 16)
            sp.dma_start(m.raw2[:, :, :], w2[0].rearrange("(c p) d -> p c d", p=P)).then_inc(late_in, 16)
            for e in range(E):
                sp.dma_start(m.b2b[:, e, :], b2[e:e + 1, :].broadcast_to([P, D])).then_inc(late_in, 16)
            sp.wait_ge(late_in, 16 * (1 + E))
            sp.wait_ge(item_free, 2 * 2 + UT)
            sp.dma_start(m.vs0[0:WIN, 1:UT, :], m.va0[WIN:P, 0:UT - 1, :]).then_inc(m.shift_in, 16)
            sp.dma_start(m.vs0[WIN:P, :, :], m.va0[0:WIN, :, :]).then_inc(m.shift_in, 16)

        @block.gpsimd
        def _(pool):
            pool.memset(m.k0[:, :, 0:WIN], 0.0)
            pool.memset(m.vs0[0:WIN, 0, :], 0.0)
            pool.memset(zeros[:, :], 0.0).then_inc(consts, 1)
            pool.memset(ones[:, :], 1.0).then_inc(consts, 1)
            pool.memset(ones_c[:, :], 1.0).then_inc(consts, 1)
            pool.wait_ge(consts, 3)
            pool.affine_select(out=tri[:, :], in_=ones[:, :], compare_op=ALU.is_gt, fill=0.0, base=0,
                               pattern=[[1, P]], channel_multiplier=-1).then_inc(consts, 1)
            it = dict(allow_small_or_imprecise_dtypes=True)
            pool.iota(iota_e[:, :], pattern=[[1, E]], base=0, channel_multiplier=0, **it).then_inc(consts, 1)
            pool.iota(iota_e8[:, :], pattern=[[1, E]], base=-E, channel_multiplier=0, **it).then_inc(consts, 1)
            pool.iota(iota_p[:, :], pattern=[[1, 1]], base=0, channel_multiplier=1, **it).then_inc(consts, 1)
            pool.iota(iota_t[:, :, :], pattern=[[0, K], [1, NT]], base=0, channel_multiplier=0, **it).then_inc(consts, 1)
            pool.iota(iota_b[:, :], pattern=[[1, P]], base=0, channel_multiplier=0, **it).then_inc(consts, 1)
            for i, (raw, high_part, low_part) in enumerate(to_split):
                pool.wait_ge(high, i + 1)
                pool.tensor_tensor(low_part[:, :, :], raw[:, :, :], high_part[:, :, :].bitcast(fp32), ALU.subtract)\
                    .then_inc(split, 1)
            for g in range(C // R):
                pool.wait_ge(hot_a, g + 1)
                if g >= 2:
                    pool.wait_ge(hot_used, g - 1)
                pool.tensor_tensor(ohV[:, g % 2, :, 0, :], ohA[:, g % 2, :, :],
                                   wide(iota_t[:, :, :].rearrange("p k t -> p (k t)"), g, E * ST), ALU.mult)\
                    .then_inc(hot_tile, 1)

        @block.scalar
        def _(act):
            act.wait_ge(sh_done, 1)
            act.activation(ex[:, :, :], shifted[:, :, :], ACT.Exp).then_inc(ex_done, 1)
            for i, (raw, high_part, _) in enumerate(to_split):
                act.wait_ge(w_in[i], 16)
                act.activation(high_part[:, :, :], raw[:, :, :], ACT.Copy).then_inc(high, 1)
                if i == 0:
                    for k in range(KD):
                        act.wait_ge(item_done, k + 1)
                        act.activation(xTh[:, k, :], psA[k][:, :], ACT.Copy).then_inc(x_high, 1)
            for n in range(4):
                act.wait_ge(item_done, KD + n + 1)
                if n % 2 == 0:
                    for s in range(2):
                        ins = act.activation(m.q0[:, n // 2, :, s, :],
                                             psA[n % 2][:, :].rearrange("p (n t) -> p n t", t=WIN),
                                             ACT.Copy, scale=m.parity[:, s:s + 1])
                else:
                    ins = act.activation(m.k0[:, n // 2, WIN:WIN + UL], psA[n % 2][:, :], ACT.Copy)
                ins.then_inc(item_free, 1)
            for g in range(C // R):
                act.wait_ge(hot_a, g + 1)
                if g >= 2:
                    act.wait_ge(hot_used, g - 1)
                act.activation(ohV[:, g % 2, :, 1, :], ohA[:, g % 2, :, :], ACT.Copy, scale=iota_p[:, 0:1])\
                    .then_inc(hot_place, 1)
                act.wait_ge(item_done, KD + 4 + g + 1)
                act.activation(m.va0[:, g, :], psA[g % 2][:, 0:D], ACT.Copy).then_inc(item_free, 1)

        @block.tensor
        def _(pe):
            pe.wait_ge(xnr_in, 16)
            for k in range(KD):
                for t in range(UT):
                    last = pe.transpose(psA[k][:, t * P:(t + 1) * P], m.xnr[:, t, k * P:(k + 1) * P], m.eye[:, :])
                last.then_inc(item_done, 1)
            pe.wait_ge(consts, 9)
            pe.wait_ge(oh_done, 1)
            flat = OHb[:, :, :].rearrange("p e c -> p (e c)")
            pe.matmul(pre_ps[:, :], tri[:, :], flat, start=True, stop=True)
            pe.matmul(tot_ps[:, :], ones[:, :], flat, start=True, stop=True).then_inc(sums_done, 1)
            pe.wait_ge(x_low, KD)
            pe.wait_ge(split, 1)
            for n in range(4):
                if n >= 2:
                    pe.wait_ge(item_free, n - 1)
                w = slice(n % 2 * D + n // 2 * P, n % 2 * D + (n // 2 + 1) * P)
                split_products(pe, psA[n % 2][:, :],
                               [(m.wqkv_h[:, k, w], m.wqkv_l[:, k, w], xTh[:, k, :], xTl[:, k, :])
                                for k in range(KD)]).then_inc(item_done, 1)
            pe.matmul(tab_ps[:, 0:2 * E * ST], zeros[:, :], zeros[:, :], start=True, stop=False)
            for g in range(C // R):
                pe.wait_ge(item_free, 4 + g - 1)
                tile, vc = slice(g * P, (g + 1) * P), slice(2 * D, 3 * D)
                split_products(pe, psA[g % 2][:, 0:D],
                               [(xTh[:, k, tile], xTl[:, k, tile], m.wqkv_h[:, k, vc], m.wqkv_l[:, k, vc])
                                for k in range(KD)]).then_inc(item_done, 1)
                for part in (hot_b, hot_tile, hot_place):
                    pe.wait_ge(part, g + 1)
                for r in range(R):
                    last = pe.matmul(tab_ps[:, 0:2 * E * ST], ohB[:, g % 2, r, :],
                                     ohV[:, g % 2, r, :, :].rearrange("p a c -> p (a c)"), start=False, stop=False)
                last.then_inc(hot_used, 1)
            pe.matmul(tab_ps[:, 0:2 * E * ST], zeros[:, :], zeros[:, :], start=False, stop=True).then_inc(tab_done, 1)

        @block.vector
        def _(dve):
            count = [0]

            def link(ins):
                count[0] += 1
                ins.then_inc(chain, 1)
                dve.wait_ge(chain, count[0])

            tokb = lambda t: t.unsqueeze(2).broadcast_to([P, NT, E])
            expb = lambda t: t.unsqueeze(1).broadcast_to([P, NT, E])
            link(dve.tensor_reduce(red[:, :], m.logits[:, :, :], AX.X, ALU.max))
            dve.tensor_tensor(shifted[:, :, :], m.logits[:, :, :], tokb(red[:, :]), ALU.subtract).then_inc(sh_done, 1)
            dve.wait_ge(ex_done, 1)
            link(dve.tensor_reduce(red[:, :], ex[:, :, :], AX.X, ALU.add))
            link(dve.reciprocal(red[:, :], red[:, :]))
            link(dve.tensor_tensor(score[:, :, :], ex[:, :, :], tokb(red[:, :]), ALU.mult))
            dve.wait_ge(consts, 9)
            for k in range(K):
                link(dve.tensor_reduce(topv[:, k, :], score[:, :, :], AX.X, ALU.max))
                link(dve.tensor_tensor(tmp[:, :, :], score[:, :, :], tokb(topv[:, k, :]), ALU.is_equal))
                link(dve.tensor_tensor(tmp2[:, :, :], tmp[:, :, :], expb(iota_e8[:, :]), ALU.mult))
                link(dve.tensor_reduce(red[:, :], tmp2[:, :, :], AX.X, ALU.min))
                oh = OH[:, :, k * NT:(k + 1) * NT].rearrange("p e t -> p t e")
                link(dve.tensor_tensor(oh, expb(iota_e8[:, :]), tokb(red[:, :]), ALU.is_equal))
                if k == 0:
                    link(dve.scalar_tensor_tensor(score[:, :, :], oh, -4.0, score[:, :, :], ALU.mult, ALU.add))
            dve.tensor_copy(OHb[:, :, :], OH[:, :, :]).then_inc(oh_done, 1)
            for k in range(KD):
                dve.wait_ge(x_high, k + 1)
                dve.tensor_tensor(xTl[:, k, :], psA[k][:, :], xTh[:, k, :].bitcast(fp32), ALU.subtract)\
                    .then_inc(x_low, 1)
            link(dve.tensor_tensor(den[:, :], topv[:, 0, :], topv[:, 1, :], ALU.add))
            link(dve.reciprocal(den[:, :], den[:, :]))
            link(dve.tensor_tensor(topv[:, :, :], topv[:, :, :], den[:, :].unsqueeze(1).broadcast_to([P, K, NT]),
                                   ALU.mult))
            link(dve.tensor_tensor(pos8[:, :, :], OH[:, :, :],
                                   iota_e[:, :].unsqueeze(2).broadcast_to([P, E, C]), ALU.mult))
            link(dve.tensor_reduce(eid[:, :], pos8[:, :, :].rearrange("p e c -> p c e"), AX.X, ALU.add))
            dve.wait_ge(sums_done, 1)
            tot = tot_ps[:, :].rearrange("p (e c) -> p e c", e=E)
            for e in range(E):
                ins = dve.tensor_tensor_scan(cum[:, e, :], ones_c[:, :], tot[:, e, :], 0.0, ALU.mult, ALU.add)
            link(ins)
            link(dve.tensor_tensor(pos8[:, :, :], cum[:, :, :], tot, ALU.subtract))
            link(dve.tensor_tensor(cum[:, :, :], pos8[:, :, :],
                                   pre_ps[:, :].rearrange("p (e c) -> p e c", e=E), ALU.add))
            link(dve.tensor_tensor(pos8[:, :, :], cum[:, :, :], OH[:, :, :], ALU.mult))
            link(dve.tensor_reduce(pos[:, :], pos8[:, :, :].rearrange("p e c -> p c e"), AX.X, ALU.add))
            link(dve.tensor_scalar(valid[:, :], pos[:, :], float(CAP), None, ALU.is_lt))
            link(dve.tensor_tensor(m.gates[:, :], topv[:, :, :].rearrange("p k t -> p (k t)"), valid[:, :], ALU.mult))
            link(dve.tensor_tensor(kept[:, :], pos[:, :], valid[:, :], ALU.mult))
            link(dve.scalar_tensor_tensor(slotf[:, :], eid[:, :], float(CAP), kept[:, :], ALU.mult, ALU.add))
            link(dve.tensor_copy(m.slots[:, :], slotf[:, :]))
            link(dve.tensor_scalar(valid[:, :], valid[:, :], -2.0 * E * CAP, 2.0 * E * CAP, ALU.mult, ALU.add))
            link(dve.tensor_tensor(dslot[:, :], slotf[:, :], valid[:, :], ALU.add))
            link(dve.tensor_copy(dint[:, :], dslot[:, :]))
            link(dve.tensor_single_scalar(aint[:, :], dint[:, :], 7, ALU.arith_shift_right))
            link(dve.tensor_single_scalar(bint[:, :], dint[:, :], P - 1, ALU.bitwise_and))
            link(dve.tensor_copy(af[:, :], aint[:, :]))
            link(dve.tensor_copy(bf[:, :], bint[:, :]))

            for g in range(C // R):
                if g >= 2:
                    dve.wait_ge(hot_used, g - 1)
                dve.tensor_tensor(ohA[:, g % 2, :, :], iota_b[:, 0:E * ST].unsqueeze(1).broadcast_to([P, R, E * ST]),
                                  wide(af, g, E * ST), ALU.is_equal).then_inc(hot_a, 1)
                dve.tensor_tensor(ohB[:, g % 2, :, :], iota_b[:, :].unsqueeze(1).broadcast_to([P, R, P]),
                                  wide(bf, g, P), ALU.is_equal).then_inc(hot_b, 1)
            dve.wait_ge(tab_done, 1)
            link(dve.tensor_copy(tabp[:, :], tab_ps[:, E * ST:2 * E * ST]))
            link(dve.scalar_tensor_tensor(m.token_of[:, :], tab_ps[:, 0:E * ST], float(P), tabp[:, :],
                                          ALU.mult, ALU.add))


def moe_phase(nc, m, xn_dram, w1, w2, y_dram):
    YR, FR = len(m.y_out), 4
    ctx = ExitStack()
    with ctx:
        sb = lambda n, s, d: ctx.enter_context(nc.sbuf_tensor(n, s, d))
        sem = lambda n: ctx.enter_context(nc.semaphore(n))
        ps = lambda n: ctx.enter_context(nc.psum_tensor(n, [P, 512], fp32))
        raw1, raw2, w1h, w1l = m.raw1, m.raw2, m.w1h, m.w1l
        w2h, w2l = sb("m_w2h", [P, HC, D], fp32r), sb("m_w2l", [P, HC, D], fp32r)
        idx = sb("m_idx", [P, ST], u32)
        xg = [sb(f"m_xg{j}", [P, D], fp32) for j in range(ST)]
        xh, xl = sb("m_xh", [P, KD, CAP], fp32r), sb("m_xl", [P, KD, CAP], fp32r)
        hf = sb("m_hf", [P, FR, HALF], fp32)
        hh, hl = sb("m_hh", [P, 2, HC, HALF], fp32r), sb("m_hl", [P, 2, HC, HALF], fp32r)
        yb = m.yb
        psF = [ps(f"m_psF{i}") for i in range(4)]
        psY = [ps(f"m_psY{i}") for i in range(2)]
        psT = [ps(f"m_psT{i}") for i in range(2)]
        raw1_in, raw2_in, xnr_in = sem("m_raw1_in"), sem("m_raw2_in"), sem("m_xnr_in")
        w1h_done, w1l_done, w2h_done, w2l_done = (sem(f"m_{n}") for n in ("w1h_d", "w1l_d", "w2h_d", "w2l_d"))
        idx_done = sem("m_idx_done")
        xg_in = [sem(f"m_xg_in{j}") for j in range(ST)]
        t_done = sem("m_t_done")
        xh_done, xl_done = sem("m_xh_done"), sem("m_xl_done")
        f_done = sem("m_f_done")
        hh_done, hl_done = sem("m_hh_done"), sem("m_hl_done")
        y_done = sem("m_y_done")
        yb_done = sem("m_yb_done")
        y_out = m.y_out
        U = 2 * HC
        TG = 2 * KD
        EARLY = {3: 0, 5: 1}
        LATE = {3: 2, 5: 3}
        w1v = w1.rearrange("e (k p) h -> p (e k) h", p=P)
        w2v = w2.rearrange("e (c p) d -> p (e c) d", p=P)
        yv = y_dram.rearrange("(s p) d -> p s d", p=P)
        block = ctx.enter_context(nc.Block())

        def experts(eng, body):
            with eng.Fori(0, E - 1) as e:
                body(e, False)
            body(E - 1, True)

        @block.sync
        def _(sp):
            ut = L // 2 // P
            sp.dma_start(m.xnr[:, :, :], xn_dram.rearrange("(t p) d -> p t d", p=P)[:, ut:2 * ut, :])\
                .then_inc(xnr_in, 16)
            sp.sem_inc(raw1_in, 16)
            sp.sem_inc(raw2_in, 16)

            def body(e, last):
                if not last:
                    alone(sp, w1h_done, e + 1)
                    alone(sp, w1l_done, e + 1)
                    sp.dma_start(raw1[:, :, :], w1v[:, bass.ds((e + 1) * KD, KD), :]).then_inc(raw1_in, 16)
                    alone(sp, w2h_done, e + 1)
                    alone(sp, w2l_done, e + 1)
                    sp.dma_start(raw2[:, :, :], w2v[:, bass.ds((e + 1) * HC, HC), :]).then_inc(raw2_in, 16)
                for s in range(ST):
                    alone(sp, yb_done, e * ST + s + 3)
                    sp.dma_start(yv[:, bass.ds(e * ST + s, 1), :], yb[:, s % YR:s % YR + 1, :]).then_inc(y_out[s % YR], 16)
            experts(sp, body)
            sp.wait_ge(xnr_in, 16)

        @block.gpsimd
        def _(pool):
            def gathers(e, first):
                if not first:
                    alone(pool, t_done, e * TG)
                pool.tensor_copy(idx[:, :], m.token_of[:, bass.ds(e * ST, ST)]).then_inc(idx_done, 1)
                alone(pool, idx_done, e + 1)
                for j in range(ST):
                    pool.indirect_dma_start(xg[j][:, :], None, xn_dram,
                                            bass.IndirectOffsetOnAxis(ap=idx[:, j:j + 1], axis=0))\
                        .then_inc(xg_in[j], 16)
            def split_w2(e, first):
                if not first:
                    alone(pool, y_done, (e + 1) * ST)
                alone(pool, raw2_in, (e + 1) * 16)
                pool.tensor_copy(w2h[:, :, :], raw2[:, :, :]).then_inc(w2h_done, 1)
                alone(pool, w2h_done, e + 1)
                pool.tensor_tensor(w2l[:, :, :], raw2[:, :, :], w2h[:, :, :].bitcast(fp32), ALU.subtract)\
                    .then_inc(w2l_done, 1)

            gathers(0, True)
            split_w2(0, True)
            with pool.Fori(1, E) as e:
                gathers(e, False)
                split_w2(e, False)

        @block.scalar
        def _(act):
            def w1_high(e):
                act.wait_ge(raw1_in, (e + 1) * 16)
                act.activation(w1h[:, :, :], raw1[:, :, :], ACT.Copy).then_inc(w1h_done, 1)

            def x_high(e, groups):
                for g in groups:
                    act.wait_ge(t_done, e * TG + g + 1)
                    act.activation(xh[:, g % KD, (g // KD) * HALF:(g // KD + 1) * HALF], psT[g % 2][:, :], ACT.Copy)\
                        .then_inc(xh_done, 1)

            act.sem_inc(w1h_done, 1)
            x_high(0, range(KD))

            def body(e, last):
                for u in range(U):
                    act.wait_ge(f_done, e * U + u + 1)
                    alone(act, hl_done, e * U + u + 1)
                    bias = m.b1T[:, bass.ds(e * HC + u % HC, 1)]
                    act.activation(hf[:, u % FR, :], psF[u % 4][:, :], ACT.Relu, bias=bias)
                    if u == 0:
                        alone(act, y_done, (e + 1) * ST)
                    act.activation(hh[:, u // HC, u % HC, :], psF[u % 4][:, :], ACT.Relu, bias=bias)\
                        .then_inc(hh_done, 1)
                    if u in LATE:
                        x_high(e, (LATE[u],))
                if not last:
                    w1_high(e + 1)
                    x_high(e + 1, range(KD))
            experts(act, body)

        @block.vector
        def _(dve):
            def w1_low(e):
                dve.wait_ge(w1h_done, e + 1)
                dve.tensor_tensor(w1l[:, :, :], raw1[:, :, :], w1h[:, :, :].bitcast(fp32), ALU.subtract)\
                    .then_inc(w1l_done, 1)

            def x_low(e, groups):
                for g in groups:
                    k, half = g % KD, g // KD
                    dve.wait_ge(xh_done, e * TG + g + 1)
                    dve.tensor_tensor(xl[:, k, half * HALF:(half + 1) * HALF], psT[g % 2][:, :],
                                      xh[:, k, half * HALF:(half + 1) * HALF].bitcast(fp32), ALU.subtract)\
                        .then_inc(xl_done, 1)

            def y_row(e, s):
                dve.wait_ge(y_done, (e + 1) * ST + s + 1)
                dve.wait_ge(y_out[s % YR], 16 * (ST // YR * e + s // YR + 1))
                dve.tensor_tensor(yb[:, s % YR:s % YR + 1, :], psY[s % 2][:, 0:D].unsqueeze(1),
                                  m.b2b[:, bass.ds(e, 1), :], ALU.add).then_inc(yb_done, 1)

            dve.sem_inc(hl_done, FR)
            dve.sem_inc(yb_done, 2)
            for r in range(YR):
                dve.sem_inc(y_out[r], 16)
            dve.sem_inc(w1l_done, 1)
            x_low(0, range(KD))

            def body(e, last):
                for u in range(U):
                    dve.wait_ge(hh_done, e * U + u + 1)
                    dve.tensor_tensor(hl[:, u // HC, u % HC, :], hf[:, u % FR, :],
                                      hh[:, u // HC, u % HC, :].bitcast(fp32), ALU.subtract).then_inc(hl_done, 1)
                    if u in LATE:
                        x_low(e, (LATE[u],))
                for s in range(ST):
                    y_row(e, s)
                    if s == 1 and not last:
                        w1_low(e + 1)
                    if s in EARLY and not last:
                        x_low(e + 1, (EARLY[s],))
            experts(dve, body)

        @block.tensor
        def _(pe):
            def transposes(e, groups):
                for g in groups:
                    k, half = g % KD, g // KD
                    pe.wait_ge(xl_done, e * TG + g + 1)
                    for j in range(ST // 2):
                        if k == 0:
                            pe.wait_ge(xg_in[half * ST // 2 + j], (e + 1) * 16)
                        last = pe.transpose(psT[g % 2][:, j * P:(j + 1) * P],
                                            xg[half * ST // 2 + j][:, k * P:(k + 1) * P], m.eye[:, :])
                    last.then_inc(t_done, 1)

            pe.sem_inc(xl_done, 2)
            pe.sem_inc(y_done, ST)
            transposes(0, range(KD))

            def body(e, last):
                pe.wait_ge(w1h_done, e + 1)
                pe.wait_ge(w1l_done, e + 1)
                for u in range(U):
                    half, c = u // HC, u % HC
                    if c == 0:
                        pe.wait_ge(xl_done, e * TG + 2 + KD * (half + 1))
                    pe.wait_ge(hl_done, e * U + u + 1)
                    cols = slice(half * HALF, (half + 1) * HALF)
                    split_products(pe, psF[u % 4][:, :],
                                   [(w1h[:, k, c * P:(c + 1) * P], w1l[:, k, c * P:(c + 1) * P],
                                     xh[:, k, cols], xl[:, k, cols]) for k in range(KD)]).then_inc(f_done, 1)
                    if u in LATE:
                        transposes(e, (LATE[u],))
                pe.wait_ge(w2h_done, e + 1)
                pe.wait_ge(w2l_done, e + 1)
                for s in range(ST):
                    half, j = s // (ST // 2), s % (ST // 2)
                    if j == 0:
                        pe.wait_ge(hl_done, e * U + FR + HC * (half + 1))
                    pe.wait_ge(yb_done, e * ST + s + 1)
                    split_products(pe, psY[s % 2][:, 0:D],
                                   [(hh[:, half, c, j * P:(j + 1) * P], hl[:, half, c, j * P:(j + 1) * P],
                                     w2h[:, c, :], w2l[:, c, :]) for c in range(HC)]).then_inc(y_done, 1)
                    if s in EARLY and not last:
                        transposes(e + 1, (EARLY[s],))
            experts(pe, body)


def attention_phase(nc, m, x, xn_dram, y_dram, out):
    UT = L // 2 // P
    UL = UT * P
    UB = UL // WIN
    BLK = 4
    STEPS = NH // 2 * UB // BLK
    UNITS = B * 2
    LAG_T, LAG_C, LAG_V, LAG_O = 3, 4, 5, 6
    LAG_I = 1
    LAG_Y = 5
    ITEMS = [("x", 0), ("x", 1), ("q", 0), ("k", 0), ("q", 1), ("k", 1)] + \
        [("o", t) for t in range(UT)] + [("v", t) for t in range(UT)]
    NI = len(ITEMS)
    O_FIRST = 2 + 2 * KD
    PRO = NI - UT
    PARTS = {"x": UT, "q": 3 * KD, "k": 3 * KD, "o": 3 * KD, "v": 3 * KD}
    COST = {"x": 0.5, "q": 1, "k": 1, "o": 0.5, "v": 0.5}
    SHARE = [4, 0, 4, 4, 4, 4, 4, 4] + [3] * 8
    parts_at, done_at = [[] for _ in range(STEPS)], [[] for _ in range(STEPS)]
    at, spent = 0, 0
    for i, (kind, _) in enumerate(ITEMS):
        for part in range(PARTS[kind]):
            while at < STEPS - 1 and spent >= sum(SHARE[:at + 1]) - 1e-6:
                at += 1
            parts_at[at].append((i, part))
            spent += COST[kind]
        done_at[at].append(i)
    PR, PTR, YG = 8, 8, 4
    GRP = 4
    ctx = ExitStack()
    with ctx:
        sb = lambda n, s, d: ctx.enter_context(nc.sbuf_tensor(n, s, d))
        sem = lambda n: ctx.enter_context(nc.semaphore(n))
        ps = lambda n: ctx.enter_context(nc.psum_tensor(n, [P, 512], fp32))
        two = lambda n: [sem(f"{n}{i}") for i in range(2)]
        xnr = m.xnr
        xTh, xTl = sb("a_xTh", [P, KD, UL], fp32r), sb("a_xTl", [P, KD, UL], fp32r)
        qz = [m.q0, sb("a_q1", [P, 2, UB, 2, WIN], fp32)]
        kT = [m.k0, sb("a_k1", [P, 2, WIN + UL], fp32)]
        va = [m.va0, sb("a_va1", [P, UT, D], fp32)]
        vs = [m.vs0, sb("a_vs1", [P, UT, D], fp32)]
        parity = m.parity
        pr = sb("a_p", [P, PR, BLK, P], fp32)
        nmax = sb("a_nmax", [P, PR, BLK], fp32)
        sums = sb("a_sums", [P, PR, BLK], fp32)
        rsum = sb("a_rsum", [P, PR, BLK], fp32)
        pT = sb("a_pT", [P, PTR, BLK, P], fp32)
        of = sb("a_o", [P, 2, BLK, WIN], fp32)
        oTh = [sb(f"a_oTh{u}", [P, KD, UL], fp32r) for u in range(2)]
        oTl = [sb(f"a_oTl{u}", [P, KD, UL], fp32r) for u in range(2)]
        res = [sb(f"a_res{u}", [P, UT, D], fp32) for u in range(2)]
        idx = [sb(f"a_idx{u}", [P, K, UT], u32) for u in range(2)]
        yg = [sb(f"a_yg{i}", [P, D], fp32) for i in range(YG)]
        psA = [ps("a_psA0"), ps("a_psA1")]
        psS = [ps("a_psS0"), ps("a_psS1")]
        psP = [ps("a_psP0"), ps("a_psP1")]
        psO = [ps("a_psO0"), ps("a_psO1")]
        xn_in = sem("a_xn_in")
        item_done, item_free = two("a_item_done"), two("a_item_free")
        x_high = sem("a_x_high")
        shift_in = m.shift_in
        s_done = two("a_s_done")
        max_done, exp_done, rsum_done, norm_done = (sem(f"a_{n}") for n in ("max", "exp", "rsum", "norm"))
        t_done, pT_done = two("a_t_done"), two("a_pT_done")
        pv_done = sem("a_pv_done")
        o_even, o_free, o_high, o_low = (sem(f"a_o_{n}") for n in ("even", "free", "high", "low"))
        res_in, res_out = two("a_res_in"), two("a_res_out")
        idx_done = sem("a_idx_done")
        yg_in = [sem(f"a_yg_in{i}") for i in range(YG)]
        acc = sem("a_acc")
        xnv = xn_dram.rearrange("(t p) d -> p t d", p=P)
        xv = x.rearrange("b (t p) d -> p (b t) d", p=P)
        ov = out.rearrange("b (t p) d -> p (b t) d", p=P)
        block = ctx.enter_context(nc.Block())
        BS, HB = 2 * STEPS, NI

        def count(b, u, i, first, last):
            n = NI * u + PRO - UT + i
            if first and u == 0 and i < O_FIRST:
                n += UT
            if last and u == 1:
                n -= O_FIRST
            return b * HB + n // 2

        def there(t, i, first, last):
            u, (kind, j) = t // STEPS, ITEMS[i]
            if kind == "o" and first and u == 0 or kind != "o" and last and u == 1:
                return None
            return u, kind, j

        def ended(t, first, last):
            if t is None or t >= BS:
                return []
            return [(i,) + there(t, i, first, last) for i in done_at[t % STEPS] if there(t, i, first, last)]

        def batches(eng, body, tail):
            body(0, True, False)
            with eng.Fori(1, B - 1) as b:
                body(b, False, False)
            body(B - 1, False, True)
            tail(B - 1)

        def lagged(t, lag, first):
            return None if first and t < lag else t - lag

        def group_out(r):
            return psO[r][:, :].rearrange("p (n s t) -> p n s t", n=BLK, s=2)

        def o_cols(parts, g):
            i = g // GRP % (STEPS // GRP)
            cols = slice((i % 2) * BLK * WIN, (i % 2 + 1) * BLK * WIN)
            return parts[g // STEPS % 2][:, i // 2, cols].rearrange("p (n t) -> p n t", n=BLK)

        @block.sync
        def _(sp):
            sp.sem_inc(xn_in, 32)
            sp.sem_inc(shift_in, 16)
            sp.dma_start(res[0][:, :, :], xv[:, 0:UT, :]).then_inc(res_in[0], 16)
            sp.dma_start(res[1][:, :, :], xv[:, UT:2 * UT, :]).then_inc(res_in[1], 16)

            def shifts(u):
                sp.dma_start(vs[u][0:WIN, 0:1, :], va[1 - u][WIN:P, UT - 1:UT, :]).then_inc(shift_in, 16)
                sp.dma_start(vs[u][0:WIN, 1:UT, :], va[u][WIN:P, 0:UT - 1, :]).then_inc(shift_in, 16)
                sp.dma_start(vs[u][WIN:P, :, :], va[u][0:WIN, :, :]).then_inc(shift_in, 16)

            def store(b, u, i, first, last):
                for j in (i - 1, i):
                    alone(sp, item_free[j % 2], count(b, u, j, first, last) + 1)
                sp.dma_start(ov[:, bass.ds(b * 2 * UT + (u - 1) * UT, UT), :], res[1 - u][:, :, :])\
                    .then_inc(res_out[1 - u], 16)

            def body(b, first, last):
                for u in range(2):
                    end = last and u == 1
                    if not last:
                        alone(sp, item_done[1], count(b, u, 1, first, last) + 1)
                        sp.dma_start(xnr[:, :, :], xnv[:, bass.ds(b * 2 * UT + (u + 2) * UT, UT), :])\
                            .then_inc(xn_in, 16)
                    if not (first and u == 0):
                        store(b, u, O_FIRST + UT - 1, first, last)
                        if not end:
                            alone(sp, res_out[1 - u], 16 * (b + u))
                            sp.dma_start(res[1 - u][:, :, :], xv[:, bass.ds(b * 2 * UT + (u + 1) * UT, UT), :])\
                                .then_inc(res_in[1 - u], 16)
                    if not end:
                        for i in (NI - 2, NI - 1):
                            alone(sp, item_free[i % 2], count(b, u, i, first, last) + 1)
                        shifts(1 - u)

            def tail(b):
                for j in (NI - 2, NI - 1):
                    sp.wait_ge(item_free[j % 2], count(b, 1, j, False, True) + 1)
                sp.dma_start(ov[:, (UNITS - 1) * UT:UNITS * UT, :], res[1][:, :, :]).then_inc(res_out[1], 16)
                for u in range(2):
                    sp.wait_ge(res_out[u], 16 * B)
            batches(sp, body, tail)

        @block.gpsimd
        def _(pool):
            slots = m.slots[:, :].rearrange("p (k t) -> p k t", k=K)
            pool.tensor_copy(idx[0][:, :, :], slots[:, :, 0:UT]).then_inc(idx_done, 1)
            for r in range(len(m.y_out)):
                pool.wait_ge(m.y_out[r], 16 * (E * ST // len(m.y_out) + 1))

            def body(b, first, last):
                for t in range(BS):
                    u, s, r = t // STEPS, t % STEPS, t % PR
                    alone(pool, rsum_done, b * BS + t + 1)
                    for j in range(BLK):
                        e = pr[:, r, j, :]
                        pool.tensor_scalar(e, e, rsum[:, r, j:j + 1], 0.0, ALU.mult, ALU.add).then_inc(norm_done, 1)
                    if s == 0:
                        alone(pool, idx_done, b * 2 + u + 1)
                    if s % 2 == 0:
                        i = s // 2
                        if not (first and u == 0 and i < YG):
                            alone(pool, acc, (b * 2 + u) * K * UT + i - YG + 1)
                        pool.indirect_dma_start(yg[i % YG][:, :], None, y_dram,
                                                bass.IndirectOffsetOnAxis(ap=idx[u][:, i % K, i // K:i // K + 1],
                                                                          axis=0)).then_inc(yg_in[i % YG], 16)
                    if s == STEPS // 2 and not (last and u == 1):
                        pool.tensor_copy(idx[1 - u][:, :, :],
                                         slots[:, :, bass.ds(b * 2 * UT + (u + 1) * UT, UT)]).then_inc(idx_done, 1)
            batches(pool, body, lambda b: None)

        @block.scalar
        def _(act):
            def read_item(kind, j, u, n, bank):
                if kind in "ko":
                    return
                act.wait_ge(item_done[bank], n + 1)
                if kind == "x":
                    act.activation(xTh[:, j, :], psA[bank][:, :], ACT.Copy).then_inc(x_high, 1)
                elif kind == "q":
                    for s in range(2):
                        ins = act.activation(qz[u][:, j, :, s, :], psA[bank][:, :].rearrange("p (n t) -> p n t", n=UB),
                                             ACT.Copy, scale=parity[:, s:s + 1])
                    ins.then_inc(item_free[bank], 1)
                else:
                    act.activation(va[u][:, j, :], psA[bank][:, 0:D], ACT.Copy).then_inc(item_free[bank], 1)

            for i in range(2):
                act.sem_inc(item_free[i], PRO // 2)
            act.sem_inc(x_high, KD)

            def steps(b, ts, first, last):
                for t in ts:
                    g = lagged(t, LAG_O, first)
                    if g is not None and g < BS and g % GRP == GRP - 1:
                        r, n = g // GRP % 2, b * (BS // GRP) + g // GRP
                        act.wait_ge(pv_done, n + 1)
                        if not (first and g < 2 * GRP):
                            act.wait_ge(o_low, n - 1)
                        act.activation(of[:, r, :, :], group_out(r)[:, :, 0, :], ACT.Copy, scale=parity[:, 0:1])\
                            .then_inc(o_even, 1)
                    g = lagged(t, LAG_O + 1, first)
                    if g is not None and g % GRP == GRP - 1:
                        act.wait_ge(o_free, b * (BS // GRP) + g // GRP + 1)
                        act.activation(o_cols(oTh, g), of[:, g // GRP % 2, :, :], ACT.Copy).then_inc(o_high, 1)
                    for i, u, kind, j in ended(lagged(t, LAG_I, first), first, last):
                        if kind == "v" and j == 0:
                            act.wait_ge(shift_in, 48 * (b * 2 + u + 1))
                            if not (first and u == 0):
                                act.wait_ge(pv_done, (b * 2 + u) * (STEPS // GRP))
                        read_item(kind, j, (1 - u) % 2, count(b, u, i, first, last), i % 2)
                    if t < BS:
                        r = t % PR
                        for j in range(BLK):
                            act.wait_ge(max_done, (b * BS + t) * BLK + j + 1)
                            e = pr[:, r, j, :]
                            act.activation(e, e, ACT.Exp, scale=-1.0, bias=nmax[:, r, j:j + 1],
                                           accum_out=sums[:, r, j:j + 1]).then_inc(exp_done, 1)

            batches(act, lambda b, first, last: steps(b, range(BS), first, last),
                    lambda b: steps(b, range(BS, BS + LAG_O + 1), False, True))

        @block.vector
        def _(dve):
            def read_item(kind, j, u, n, bank, xh_count):
                if kind == "x":
                    dve.wait_ge(x_high, xh_count)
                    dve.tensor_tensor(xTl[:, j, :], psA[bank][:, :], xTh[:, j, :].bitcast(fp32), ALU.subtract)\
                        .then_inc(item_free[bank], 1)
                elif kind == "k":
                    dve.tensor_copy(kT[u][:, j, 0:WIN], kT[1 - u][:, j, UL:UL + WIN])
                    dve.wait_ge(item_done[bank], n + 1)
                    dve.tensor_copy(kT[u][:, j, WIN:WIN + UL], psA[bank][:, :]).then_inc(item_free[bank], 1)

            def steps(b, ts, first, last):
                for t in ts:
                    if t < BS:
                        r = t % PR
                        if not (first and t < PR):
                            dve.wait_ge(t_done[t % 2], b * STEPS + (t - PR) // 2 + 1)
                        alone(dve, s_done[t % 2], b * STEPS + t // 2 + 1)
                        for j in range(BLK):
                            band = 1 if t < STEPS and t // GRP % 2 == 0 and j == 0 else 0
                            dve.tensor_tensor_reduce(
                                out=pr[:, r, j, :], in0=psS[t % 2][:, j * P:(j + 1) * P],
                                in1=m.mask[:, band, :], scale=-(DH ** -0.5), scalar=BIG,
                                op0=ALU.add, op1=ALU.min, accum_out=nmax[:, r, j:j + 1]).then_inc(max_done, 1)
                    g = lagged(t, 1, first)
                    if g is not None and g < BS:
                        dve.wait_ge(exp_done, (b * BS + g + 1) * BLK)
                        dve.reciprocal(rsum[:, g % PR, :], sums[:, g % PR, :]).then_inc(rsum_done, 1)
                    g = lagged(t, LAG_C, first)
                    if g is not None and g < BS:
                        dve.wait_ge(t_done[g % 2], b * STEPS + g // 2 + 1)
                        if not (first and g < PTR):
                            dve.wait_ge(pv_done, b * (BS // GRP) + (g - PTR) // GRP + 1)
                        dve.tensor_copy(pT[:, g % PTR, :, :].rearrange("p c q -> p (c q)"), psP[g % 2][:, :])\
                            .then_inc(pT_done[g % 2], 1)
                    for i, u, kind, j in ended(lagged(t, LAG_I, first), first, last):
                        n = count(b, u, i, first, last)
                        if kind == "o":
                            add_out((1 - u) % 2, j, n, i % 2, (b * 2 + u) * K * UT)
                        else:
                            read_item(kind, j, (1 - u) % 2, n, i % 2, (b * 2 + u + 1) * KD + j + 1)
                    g = lagged(t, LAG_Y, first)
                    if g is not None and g < BS and g % 2 == 0:
                        u, i = g // STEPS % 2, g % STEPS // 2
                        ub = b * 2 + g // STEPS
                        tile, k = i // K, i % K
                        if i == 0:
                            dve.wait_ge(res_in[u], 16 * (b + (g // STEPS + 2) // 2))
                        dve.wait_ge(yg_in[i % YG], 16 * (ub * (K * UT // YG) + i // YG + 1))
                        if k == 1:
                            dve.wait_ge(acc, ub * K * UT + i)
                        dve.scalar_tensor_tensor(res[u][:, tile, :], yg[i % YG][:, :],
                                                 m.gates[:, bass.ds(ub * UT + k * NT + tile, 1)],
                                                 res[u][:, tile, :], ALU.mult, ALU.add).then_inc(acc, 1)
                    g = lagged(t, LAG_O, first)
                    if g is not None and g < BS and g % GRP == GRP - 1:
                        r = g // GRP % 2
                        dve.wait_ge(o_even, b * (BS // GRP) + g // GRP + 1)
                        dve.scalar_tensor_tensor(of[:, r, :, :], group_out(r)[:, :, 1, :], parity[:, 1:2],
                                                 of[:, r, :, :], ALU.mult, ALU.add).then_inc(o_free, 1)
                    g = lagged(t, LAG_O + 1, first)
                    if g is not None and g % GRP == GRP - 1:
                        dve.wait_ge(o_high, b * (BS // GRP) + g // GRP + 1)
                        dve.tensor_tensor(o_cols(oTl, g), of[:, g // GRP % 2, :, :], o_cols(oTh, g).bitcast(fp32),
                                          ALU.subtract).then_inc(o_low, 1)

            def add_out(u, j, n, bank, sums_before):
                dve.wait_ge(acc, sums_before)
                dve.wait_ge(item_done[bank], n + 1)
                dve.tensor_tensor(res[u][:, j, :], res[u][:, j, :], psA[bank][:, 0:D], ALU.add)\
                    .then_inc(item_free[bank], 1)

            def tail(b):
                steps(b, range(BS, BS + LAG_O + 1), False, True)
                for j in range(UT):
                    add_out(1, j, count(b, 1, NI - UT + j, False, True), j % 2, UNITS * K * UT)
            batches(dve, lambda b, first, last: steps(b, range(BS), first, last), tail)

        @block.tensor
        def _(pe):
            def product(kind, j, u, n, bank, xn_count, o_count, parts):
                begins = parts[0] == 0
                if begins:
                    pe.wait_ge(item_free[bank], n)
                if begins and kind == "x":
                    pe.wait_ge(xn_in, xn_count)
                if begins and kind == "q" and j == 0:
                    pe.wait_ge(item_free[1 - bank], n)
                if begins and kind == "o" and j == 0:
                    pe.wait_ge(o_low, o_count)
                out_ps = psA[bank]
                tile = slice(j * P, (j + 1) * P)
                for part in parts:
                    if kind == "x":
                        last = pe.transpose(out_ps[:, part * P:(part + 1) * P], xnr[:, part, j * P:(j + 1) * P],
                                            m.eye[:, :])
                        continue
                    k, low_l, low_r = part // 3, part % 3 == 2, part % 3 == 1
                    w = {"q": slice(j * P, (j + 1) * P), "k": slice(D + j * P, D + (j + 1) * P),
                         "v": slice(2 * D, 3 * D), "o": slice(0, D)}[kind]
                    wqkv = lambda low: (m.wqkv_l if low else m.wqkv_h)[:, k, w]
                    xT = lambda low: xTl if low else xTh
                    if kind in "qk":
                        args = out_ps[:, :], wqkv(low_l), xT(low_r)[:, k, :]
                    elif kind == "v":
                        args = out_ps[:, 0:D], xT(low_l)[:, k, tile], wqkv(low_r)
                    else:
                        args = out_ps[:, 0:D], (oTl if low_l else oTh)[u][:, k, tile], \
                            (m.wout_l if low_r else m.wout_h)[:, k, w]
                    last = pe.matmul(*args, start=part == 0, stop=part == 3 * KD - 1)
                if parts[-1] == PARTS[kind] - 1:
                    last.then_inc(item_done[bank], 1)

            for i in range(2):
                pe.sem_inc(item_done[i], PRO // 2)

            def scores(b, t, first):
                u, s = t // STEPS % 2, t % STEPS
                mt, half, rows = s // (2 * GRP), s // GRP % 2, slice(32 * (s % GRP), 32 * (s % GRP) + 32)
                if s == 0:
                    for i in (O_FIRST - 2, O_FIRST - 1):
                        pe.wait_ge(item_free[i % 2], i // 2 + 1 if first and t == 0 else
                                   count(b, t // STEPS - 1, i, first, False) + 1)
                if not (first and t < 2):
                    pe.wait_ge(max_done, (b * BS + t - 1) * BLK)
                for j in range(BLK):
                    blk = half * BLK + j
                    ins = pe.matmul(psS[t % 2][:, j * P:(j + 1) * P],
                                    qz[u][rows, mt, blk, :, :].rearrange("p s t -> p (s t)"),
                                    kT[u][rows, mt, blk * WIN:blk * WIN + 2 * WIN], start=True, stop=True)
                ins.then_inc(s_done[t % 2], 1)

            def steps(b, ts, first, last):
                for t in ts:
                    if t < BS - 1 or t == BS - 1 and not last:
                        scores(b, t + 1, first)
                    g = lagged(t, LAG_T, first)
                    if g is not None and g < BS:
                        pe.wait_ge(norm_done, (b * BS + g + 1) * BLK)
                        if not (first and g < 2):
                            pe.wait_ge(pT_done[g % 2], b * STEPS + g // 2)
                        for j in range(BLK):
                            ins = pe.transpose(psP[g % 2][:, j * P:(j + 1) * P], pr[:, g % PR, j, :], m.eye[:, :])
                        ins.then_inc(t_done[g % 2], 1)
                    g = lagged(t, LAG_V, first)
                    if g is not None and g < BS and g % GRP == GRP - 1:
                        s, r, n = g % STEPS, g // GRP % 2, b * (BS // GRP) + g // GRP
                        mt, half = s // (2 * GRP), s // GRP % 2
                        if s == GRP - 1:
                            pe.wait_ge(shift_in, 48 * (b * 2 + g // STEPS + 1))
                        for i in (0, 1):
                            pe.wait_ge(pT_done[i], b * STEPS + g // 2 + 1)
                        if not (first and g < 2 * GRP):
                            pe.wait_ge(o_free, n - 1)
                        for j in range(BLK):
                            blk = half * BLK + j
                            v = (va if blk % 2 else vs)[g // STEPS % 2]
                            for c in range(GRP):
                                heads = slice(mt * P + 32 * c, mt * P + 32 * (c + 1))
                                ins = pe.matmul(psO[r][32 * c:32 * (c + 1), j * P:(j + 1) * P],
                                                v[:, blk // 2, heads], pT[:, (g - GRP + 1 + c) % PTR, j, :],
                                                start=True, stop=True)
                        ins.then_inc(pv_done, 1)
                    if t < BS:
                        for i in range(NI):
                            parts = [part for item, part in parts_at[t % STEPS] if item == i]
                            if parts and there(t, i, first, last):
                                u, kind, j = there(t, i, first, last)
                                product(kind, j, 1 - u, count(b, u, i, first, last), i % 2,
                                        16 * (b * 2 + u + 2), (b * 2 + u) * (STEPS // GRP), parts)

            scores(0, 0, True)

            def tail(b):
                steps(b, range(BS, BS + LAG_V + 1), False, True)
                for j in range(UT):
                    product("o", j, 1, count(b, 1, NI - UT + j, False, True), j % 2, 0, B * (BS // GRP), range(3 * KD))
            batches(pe, lambda b, first, last: steps(b, range(BS), first, last), tail)


def build(nc, x, w_qkv, w_out, wg, w1, b1, w2, b2, out):
    ctx = ExitStack()
    with ctx:
        sb = lambda n, s, d: ctx.enter_context(nc.sbuf_tensor(n, s, d))
        xn_dram = nc.dram_tensor("xn_scratch", (N, D), fp32, kind="Internal").ap()
        y_dram = nc.dram_tensor("y_scratch", (E * CAP, D), fp32, kind="Internal").ap()
        m = Mem()
        Mem.passed = ctx.enter_context(nc.semaphore("waits_passed"))
        m.eye = sb("eye", [P, P], fp32)
        m.mask = sb("mask", [P, 2, 2 * WIN], fp32)
        m.logits = sb("logits", [P, NT, E], fp32)
        m.wqkv_h, m.wqkv_l = sb("wqkv_h", [P, KD, 3 * D], fp32r), sb("wqkv_l", [P, KD, 3 * D], fp32r)
        m.wout_h, m.wout_l = sb("wout_h", [P, KD, D], fp32r), sb("wout_l", [P, KD, D], fp32r)
        m.gates = sb("gates", [P, K * NT], fp32)
        m.slots = sb("slots", [P, K * NT], u32)
        m.token_of = sb("token_of", [P, E * ST], u32)
        m.yb = sb("y", [P, 4, D], fp32)
        m.y_out = [ctx.enter_context(nc.semaphore(f"y_out{i}")) for i in range(4)]
        tiles, tokens = L // 2 // P, L // 2
        m.xnr, m.va0, m.vs0 = (sb(n, [P, tiles, D], fp32) for n in ("xnr", "va0", "vs0"))
        m.q0 = sb("q0", [P, 2, tokens // WIN, 2, WIN], fp32)
        m.k0 = sb("k0", [P, 2, WIN + tokens], fp32)
        m.parity = sb("parity", [P, 2], fp32)
        m.shift_in = ctx.enter_context(nc.semaphore("shift_in"))
        with ExitStack() as inner:
            m.b1T = inner.enter_context(nc.sbuf_tensor("b1T", [P, E * HC], fp32))
            m.b2b = inner.enter_context(nc.sbuf_tensor("b2b", [P, E, D], fp32))
            m.raw1 = inner.enter_context(nc.sbuf_tensor("raw1", [P, KD, H], fp32))
            m.raw2 = inner.enter_context(nc.sbuf_tensor("raw2", [P, HC, D], fp32))
            m.w1h = inner.enter_context(nc.sbuf_tensor("w1h", [P, KD, H], fp32r))
            m.w1l = inner.enter_context(nc.sbuf_tensor("w1l", [P, KD, H], fp32r))
            with ExitStack() as early:
                m.raw_qkv = early.enter_context(nc.sbuf_tensor("raw_qkv", [P, KD, 3 * D], fp32))
                m.raw_out = early.enter_context(nc.sbuf_tensor("raw_out", [P, KD, D], fp32))
                norm_phase(nc, m, x, xn_dram, wg, b1)
                route_phase(nc, m, xn_dram, w_qkv, w_out, w1, w2, b2)
            moe_phase(nc, m, xn_dram, w1, w2, y_dram)
        attention_phase(nc, m, x, xn_dram, y_dram, out)


_INS = ['L0_attn_x', 'L0_attn_w_qkv', 'L0_attn_w_out', 'L0_ffn_wg', 'L0_ffn_w1', 'L0_ffn_b1', 'L0_ffn_w2',
        'L0_ffn_b2']


def kernel(**inputs):
    import numpy as _np
    import concourse.bacc as _bacc
    from concourse import mybir as _mybir
    from concourse.bass_utils import run_bass_kernel_spmd as _run

    nc = _bacc.Bacc("TRN2", target_bir_lowering=False, num_devices=1)
    arrays, args = {}, []
    for name in _INS:
        a = _np.ascontiguousarray(inputs[name])
        arrays[f"in_{name}"] = a
        args.append(nc.dram_tensor(f"in_{name}", a.shape, _mybir.dt.from_np(a.dtype), kind="ExternalInput").ap())
    o = nc.dram_tensor("out_0", (B, L, D), fp32, kind="ExternalOutput").ap()
    build(nc, *args, o)
    r = _run(nc, [arrays], core_ids=[0])
    return r.results[0]["out_0"]
```
